# Optimizing a Trainium2 kernel written in Bass

```python
import numpy as np
import jax
import jax.numpy as jnp

def _softmax(x, axis=-1):
    return jax.nn.softmax(x, axis=axis)

def _gelu(x):
    return jax.nn.gelu(x, approximate=True)

def _silu(x):
    return jax.nn.silu(x)

def _sigmoid(x):
    return jax.nn.sigmoid(x)

def _layernorm(x, axis=-1, eps=1e-05):
    m = jnp.mean(x, axis=axis, keepdims=True)
    v = jnp.var(x, axis=axis, keepdims=True)
    return (x - m) / jnp.sqrt(v + eps)

def _scatter_add(tgt, idx, src, axis=0):
    return tgt.at[idx].add(src)

def _segment_sum(src, seg, n):
    return jax.ops.segment_sum(src, seg, n)
kernel_name = 'mk_rec_standalone_d1_rec_r8_c40054'

def setup_inputs(seed: int=0):
    np.random.seed(seed)
    _w = jnp.asarray

    def _rec_inputs():
        import jax
        import jax.numpy as jnp
        _rk = jax.random.key(seed)
        r_user_features = jax.random.randint(jax.random.fold_in(_rk, 1), (512, 1), 72, 99964, jnp.int32)
        r_candidate_features = jax.random.randint(jax.random.fold_in(_rk, 2), (512, 1), 20, 19995, jnp.int32)
        r_recent_features = jnp.stack([jax.random.randint(jax.random.fold_in(jax.random.fold_in(_rk, 3), 0), (512,), 11, 19998, jnp.int32), jax.random.randint(jax.random.fold_in(jax.random.fold_in(_rk, 3), 1), (512,), 2, 19993, jnp.int32), jax.random.randint(jax.random.fold_in(jax.random.fold_in(_rk, 3), 2), (512,), 7, 2500, jnp.int32), jax.random.randint(jax.random.fold_in(jax.random.fold_in(_rk, 3), 3), (512,), 3, 19999, jnp.int32), jax.random.randint(jax.random.fold_in(jax.random.fold_in(_rk, 3), 4), (512,), 1, 2500, jnp.int32), jax.random.randint(jax.random.fold_in(jax.random.fold_in(_rk, 3), 5), (512,), 2, 2500, jnp.int32), jax.random.randint(jax.random.fold_in(jax.random.fold_in(_rk, 3), 6), (512,), 8, 2500, jnp.int32), jax.random.randint(jax.random.fold_in(jax.random.fold_in(_rk, 3), 7), (512,), 0, 19995, jnp.int32), jax.random.randint(jax.random.fold_in(jax.random.fold_in(_rk, 3), 8), (512,), 2, 19998, jnp.int32), jax.random.randint(jax.random.fold_in(jax.random.fold_in(_rk, 3), 9), (512,), 1, 2500, jnp.int32), jax.random.randint(jax.random.fold_in(jax.random.fold_in(_rk, 3), 10), (512,), 5, 19997, jnp.int32), jax.random.randint(jax.random.fold_in(jax.random.fold_in(_rk, 3), 11), (512,), 1, 2500, jnp.int32), jax.random.randint(jax.random.fold_in(jax.random.fold_in(_rk, 3), 12), (512,), 0, 2500, jnp.int32), jax.random.randint(jax.random.fold_in(jax.random.fold_in(_rk, 3), 13), (512,), 12, 2500, jnp.int32), jax.random.randint(jax.random.fold_in(jax.random.fold_in(_rk, 3), 14), (512,), 0, 19999, jnp.int32), jax.random.randint(jax.random.fold_in(jax.random.fold_in(_rk, 3), 15), (512,), 4, 19995, jnp.int32), jax.random.randint(jax.random.fold_in(jax.random.fold_in(_rk, 3), 16), (512,), 1, 19989, jnp.int32), jax.random.randint(jax.random.fold_in(jax.random.fold_in(_rk, 3), 17), (512,), 5, 19997, jnp.int32), jax.random.randint(jax.random.fold_in(jax.random.fold_in(_rk, 3), 18), (512,), 1, 19997, jnp.int32), jax.random.randint(jax.random.fold_in(jax.random.fold_in(_rk, 3), 19), (512,), 3, 19994, jnp.int32), jax.random.randint(jax.random.fold_in(jax.random.fold_in(_rk, 3), 20), (512,), 10, 19993, jnp.int32), jax.random.randint(jax.random.fold_in(jax.random.fold_in(_rk, 3), 21), (512,), 1, 2500, jnp.int32), jax.random.randint(jax.random.fold_in(jax.random.fold_in(_rk, 3), 22), (512,), 2, 19999, jnp.int32), jax.random.randint(jax.random.fold_in(jax.random.fold_in(_rk, 3), 23), (512,), 15, 2500, jnp.int32), jax.random.randint(jax.random.fold_in(jax.random.fold_in(_rk, 3), 24), (512,), 3, 2500, jnp.int32), jax.random.randint(jax.random.fold_in(jax.random.fold_in(_rk, 3), 25), (512,), 8, 19998, jnp.int32), jax.random.randint(jax.random.fold_in(jax.random.fold_in(_rk, 3), 26), (512,), 0, 19995, jnp.int32), jax.random.randint(jax.random.fold_in(jax.random.fold_in(_rk, 3), 27), (512,), 1, 19998, jnp.int32), jax.random.randint(jax.random.fold_in(jax.random.fold_in(_rk, 3), 28), (512,), 11, 19999, jnp.int32), jax.random.randint(jax.random.fold_in(jax.random.fold_in(_rk, 3), 29), (512,), 2, 2499, jnp.int32), jax.random.randint(jax.random.fold_in(jax.random.fold_in(_rk, 3), 30), (512,), 1, 19999, jnp.int32), jax.random.randint(jax.random.fold_in(jax.random.fold_in(_rk, 3), 31), (512,), 3, 19996, jnp.int32), jax.random.randint(jax.random.fold_in(jax.random.fold_in(_rk, 3), 32), (512,), 3, 2500, jnp.int32), jax.random.randint(jax.random.fold_in(jax.random.fold_in(_rk, 3), 33), (512,), 2, 19999, jnp.int32), jax.random.randint(jax.random.fold_in(jax.random.fold_in(_rk, 3), 34), (512,), 6, 19997, jnp.int32), jax.random.randint(jax.random.fold_in(jax.random.fold_in(_rk, 3), 35), (512,), 2, 19995, jnp.int32), jax.random.randint(jax.random.fold_in(jax.random.fold_in(_rk, 3), 36), (512,), 0, 19986, jnp.int32), jax.random.randint(jax.random.fold_in(jax.random.fold_in(_rk, 3), 37), (512,), 4, 19998, jnp.int32), jax.random.randint(jax.random.fold_in(jax.random.fold_in(_rk, 3), 38), (512,), 1, 19997, jnp.int32), jax.random.randint(jax.random.fold_in(jax.random.fold_in(_rk, 3), 39), (512,), 6, 19971, jnp.int32), jax.random.randint(jax.random.fold_in(jax.random.fold_in(_rk, 3), 40), (512,), 5, 19995, jnp.int32), jax.random.randint(jax.random.fold_in(jax.random.fold_in(_rk, 3), 41), (512,), 0, 2500, jnp.int32), jax.random.randint(jax.random.fold_in(jax.random.fold_in(_rk, 3), 42), (512,), 0, 19998, jnp.int32), jax.random.randint(jax.random.fold_in(jax.random.fold_in(_rk, 3), 43), (512,), 2, 2500, jnp.int32), jax.random.randint(jax.random.fold_in(jax.random.fold_in(_rk, 3), 44), (512,), 0, 2499, jnp.int32), jax.random.randint(jax.random.fold_in(jax.random.fold_in(_rk, 3), 45), (512,), 5, 19999, jnp.int32), jax.random.randint(jax.random.fold_in(jax.random.fold_in(_rk, 3), 46), (512,), 0, 19997, jnp.int32), jax.random.randint(jax.random.fold_in(jax.random.fold_in(_rk, 3), 47), (512,), 5, 19999, jnp.int32), jax.random.randint(jax.random.fold_in(jax.random.fold_in(_rk, 3), 48), (512,), 0, 2500, jnp.int32), jax.random.randint(jax.random.fold_in(jax.random.fold_in(_rk, 3), 49), (512,), 6, 19998, jnp.int32)], axis=1)
        return (r_user_features, r_candidate_features, r_recent_features)
    r_user_features, r_candidate_features, r_recent_features = _rec_inputs()

    def _L0_rec_setup():
        import jax, jax.numpy as jnp
        import numpy as np
        B, T, D, H, C, U = (512, 50, 128, 128, 2500, 12500)
        H1, H2 = (128, 64)

        def _prelu(x, a):
            return jnp.where(x >= 0, x, a * x)

        def _bn(x, g, b):
            m = jnp.mean(x, axis=0)
            v = jnp.mean((x - m) ** 2, axis=0)
            return (x - m) / jnp.sqrt(v + 1e-05) * g + b
        key = jax.random.key(seed)
        ks = jax.random.split(key, 40)
        g = lambda i, shape, s=0.05: jax.random.normal(ks[i], shape, dtype=jnp.float32) * s
        a0 = jnp.array(0.25, dtype=jnp.float32)
        return {'user_features': jax.random.randint(ks[0], (B, 1), 0, U), 'candidate_features': jax.random.randint(ks[1], (B, 1), 0, C), 'recent_features': jax.random.randint(ks[2], (B, T), 0, C), 'user_emb': g(3, (U, D)), 'cand_emb': g(4, (C, D)), 'recent_emb': g(5, (T, C, D)), 'gru_W_ih': g(6, (3 * D, D)), 'gru_W_hh': g(7, (3 * D, D)), 'gru_b_ih': g(8, (3 * D,)), 'gru_b_hh': g(9, (3 * D,)), 'att_W1': g(10, (4 * D, 32)), 'att_b1': g(11, (32,)), 'att_a1': a0, 'att_W2': g(12, (32, 32)), 'att_b2': g(13, (32,)), 'att_a2': a0, 'att_W3': g(14, (32, 1)), 'att_b3': g(15, (1,)), 'aug_Wr': g(16, (D + H, H)), 'aug_br': g(17, (H,)), 'aug_Wu': g(18, (D + H, H)), 'aug_bu': g(19, (H,)), 'aug_Wh': g(20, (D + H, H)), 'aug_bh': g(21, (H,)), 'dnn_W1': g(22, (2 * D + H, H1)), 'dnn_b1': g(23, (H1,)), 'bn1_g': jnp.ones((H1,), jnp.float32), 'bn1_b': jnp.zeros((H1,), jnp.float32), 'dnn_a1': a0, 'dnn_W2': g(24, (H1, H2)), 'dnn_b2': g(25, (H2,)), 'bn2_g': jnp.ones((H2,), jnp.float32), 'bn2_b': jnp.zeros((H2,), jnp.float32), 'dnn_a2': a0, 'dnn_W3': g(26, (H2, 1)), 'dnn_b3': g(27, (1,))}
    _L0_rec_all = _L0_rec_setup()
    _L0_rec_in = {k: v for k, v in _L0_rec_all.items() if k in ('user_emb', 'cand_emb', 'recent_emb', 'gru_W_ih', 'gru_W_hh', 'gru_b_ih', 'gru_b_hh', 'att_W1', 'att_b1', 'att_a1', 'att_W2', 'att_b2', 'att_a2', 'att_W3', 'att_b3', 'aug_Wr', 'aug_br', 'aug_Wu', 'aug_bu', 'aug_Wh', 'aug_bh', 'dnn_W1', 'dnn_b1', 'bn1_g', 'bn1_b', 'dnn_a1', 'dnn_W2', 'dnn_b2', 'bn2_g', 'bn2_b', 'dnn_a2', 'dnn_W3', 'dnn_b3')}
    del _L0_rec_all
    return {'r_user_features': r_user_features, 'r_candidate_features': r_candidate_features, 'r_recent_features': r_recent_features, 'L0_rec_user_emb': _L0_rec_in['user_emb'], 'L0_rec_cand_emb': _L0_rec_in['cand_emb'], 'L0_rec_recent_emb': _L0_rec_in['recent_emb'], 'L0_rec_gru_W_ih': _L0_rec_in['gru_W_ih'], 'L0_rec_gru_W_hh': _L0_rec_in['gru_W_hh'], 'L0_rec_gru_b_ih': _L0_rec_in['gru_b_ih'], 'L0_rec_gru_b_hh': _L0_rec_in['gru_b_hh'], 'L0_rec_att_W1': _L0_rec_in['att_W1'], 'L0_rec_att_b1': _L0_rec_in['att_b1'], 'L0_rec_att_a1': _L0_rec_in['att_a1'], 'L0_rec_att_W2': _L0_rec_in['att_W2'], 'L0_rec_att_b2': _L0_rec_in['att_b2'], 'L0_rec_att_a2': _L0_rec_in['att_a2'], 'L0_rec_att_W3': _L0_rec_in['att_W3'], 'L0_rec_att_b3': _L0_rec_in['att_b3'], 'L0_rec_aug_Wr': _L0_rec_in['aug_Wr'], 'L0_rec_aug_br': _L0_rec_in['aug_br'], 'L0_rec_aug_Wu': _L0_rec_in['aug_Wu'], 'L0_rec_aug_bu': _L0_rec_in['aug_bu'], 'L0_rec_aug_Wh': _L0_rec_in['aug_Wh'], 'L0_rec_aug_bh': _L0_rec_in['aug_bh'], 'L0_rec_dnn_W1': _L0_rec_in['dnn_W1'], 'L0_rec_dnn_b1': _L0_rec_in['dnn_b1'], 'L0_rec_bn1_g': _L0_rec_in['bn1_g'], 'L0_rec_bn1_b': _L0_rec_in['bn1_b'], 'L0_rec_dnn_a1': _L0_rec_in['dnn_a1'], 'L0_rec_dnn_W2': _L0_rec_in['dnn_W2'], 'L0_rec_dnn_b2': _L0_rec_in['dnn_b2'], 'L0_rec_bn2_g': _L0_rec_in['bn2_g'], 'L0_rec_bn2_b': _L0_rec_in['bn2_b'], 'L0_rec_dnn_a2': _L0_rec_in['dnn_a2'], 'L0_rec_dnn_W3': _L0_rec_in['dnn_W3'], 'L0_rec_dnn_b3': _L0_rec_in['dnn_b3']}

def reference(r_user_features, r_candidate_features, r_recent_features, L0_rec_user_emb, L0_rec_cand_emb, L0_rec_recent_emb, L0_rec_gru_W_ih, L0_rec_gru_W_hh, L0_rec_gru_b_ih, L0_rec_gru_b_hh, L0_rec_att_W1, L0_rec_att_b1, L0_rec_att_a1, L0_rec_att_W2, L0_rec_att_b2, L0_rec_att_a2, L0_rec_att_W3, L0_rec_att_b3, L0_rec_aug_Wr, L0_rec_aug_br, L0_rec_aug_Wu, L0_rec_aug_bu, L0_rec_aug_Wh, L0_rec_aug_bh, L0_rec_dnn_W1, L0_rec_dnn_b1, L0_rec_bn1_g, L0_rec_bn1_b, L0_rec_dnn_a1, L0_rec_dnn_W2, L0_rec_dnn_b2, L0_rec_bn2_g, L0_rec_bn2_b, L0_rec_dnn_a2, L0_rec_dnn_W3, L0_rec_dnn_b3):
    import jax
    import jax.numpy as jnp

    def _L0_rec_ref(user_features, candidate_features, recent_features, user_emb, cand_emb, recent_emb, gru_W_ih, gru_W_hh, gru_b_ih, gru_b_hh, att_W1, att_b1, att_a1, att_W2, att_b2, att_a2, att_W3, att_b3, aug_Wr, aug_br, aug_Wu, aug_bu, aug_Wh, aug_bh, dnn_W1, dnn_b1, bn1_g, bn1_b, dnn_a1, dnn_W2, dnn_b2, bn2_g, bn2_b, dnn_a2, dnn_W3, dnn_b3):
        import jax, jax.numpy as jnp
        import numpy as np
        B, T, D, H, C, U = (512, 50, 128, 128, 2500, 12500)
        H1, H2 = (128, 64)

        def _prelu(x, a):
            return jnp.where(x >= 0, x, a * x)

        def _bn(x, g, b):
            m = jnp.mean(x, axis=0)
            v = jnp.mean((x - m) ** 2, axis=0)
            return (x - m) / jnp.sqrt(v + 1e-05) * g + b
        b = user_features.shape[0]
        d = user_emb.shape[1]
        hdim = aug_br.shape[0]
        u_e = user_emb[user_features[:, 0]]
        c_e = cand_emb[candidate_features[:, 0]]
        r_e = jax.vmap(lambda tab, ids: tab[ids], in_axes=(0, 1), out_axes=0)(recent_emb, recent_features)

        def gru_step(h, x):
            gi = x @ gru_W_ih.T + gru_b_ih
            gh = h @ gru_W_hh.T + gru_b_hh
            i_r, i_z, i_n = jnp.split(gi, 3, axis=1)
            h_r, h_z, h_n = jnp.split(gh, 3, axis=1)
            r = jax.nn.sigmoid(i_r + h_r)
            z = jax.nn.sigmoid(i_z + h_z)
            n = jnp.tanh(i_n + r * h_n)
            h_new = (1 - z) * n + z * h
            return (h_new, h_new)
        _, hs = jax.lax.scan(gru_step, jnp.zeros((b, d), jnp.float32), r_e)
        cand_t = jnp.broadcast_to(c_e[None, :, :], hs.shape)
        unit = jnp.concatenate([hs, cand_t, hs - cand_t, hs * cand_t], axis=-1)
        a = _prelu(unit @ att_W1 + att_b1, att_a1)
        a = _prelu(a @ att_W2 + att_b2, att_a2)
        att = jax.nn.sigmoid(a @ att_W3 + att_b3)

        def aug_step(h, xa):
            x, s = xa
            cat = jnp.concatenate([x, h], axis=1)
            r = jax.nn.sigmoid(cat @ aug_Wr + aug_br)
            u = jax.nn.sigmoid(cat @ aug_Wu + aug_bu)
            h_hat = jnp.tanh(jnp.concatenate([r * h, x], axis=1) @ aug_Wh + aug_bh)
            u = s * u
            h_new = (1 - u) * h + u * h_hat
            return (h_new, None)
        h_final, _ = jax.lax.scan(aug_step, jnp.zeros((b, hdim), jnp.float32), (hs, att))
        z1 = _prelu(_bn(jnp.concatenate([u_e, c_e, h_final], axis=1) @ dnn_W1 + dnn_b1, bn1_g, bn1_b), dnn_a1)
        z2 = _prelu(_bn(z1 @ dnn_W2 + dnn_b2, bn2_g, bn2_b), dnn_a2)
        return z2 @ dnn_W3 + dnn_b3
    y = _L0_rec_ref(r_user_features, r_candidate_features, r_recent_features, L0_rec_user_emb, L0_rec_cand_emb, L0_rec_recent_emb, L0_rec_gru_W_ih, L0_rec_gru_W_hh, L0_rec_gru_b_ih, L0_rec_gru_b_hh, L0_rec_att_W1, L0_rec_att_b1, L0_rec_att_a1, L0_rec_att_W2, L0_rec_att_b2, L0_rec_att_a2, L0_rec_att_W3, L0_rec_att_b3, L0_rec_aug_Wr, L0_rec_aug_br, L0_rec_aug_Wu, L0_rec_aug_bu, L0_rec_aug_Wh, L0_rec_aug_bh, L0_rec_dnn_W1, L0_rec_dnn_b1, L0_rec_bn1_g, L0_rec_bn1_b, L0_rec_dnn_a1, L0_rec_dnn_W2, L0_rec_dnn_b2, L0_rec_bn2_g, L0_rec_bn2_b, L0_rec_dnn_a2, L0_rec_dnn_W3, L0_rec_dnn_b3)
    return y

_drawn_inputs = setup_inputs


def setup_inputs(seed=0):
    import zlib

    import numpy as np

    out = dict(_drawn_inputs(seed))
    spreads = {'L0_rec_bn1_g': (1.0, 0.2),
     'L0_rec_bn1_b': (0.0, 0.305),
     'L0_rec_bn2_g': (1.0, 0.2),
     'L0_rec_bn2_b': (0.0, 0.1)}
    factors = {'L0_rec_gru_b_ih': 8.0,
     'L0_rec_gru_b_hh': 8.0,
     'L0_rec_att_W1': 8.0,
     'L0_rec_att_b1': 8.0,
     'L0_rec_att_W2': 8.0,
     'L0_rec_att_b2': 8.0,
     'L0_rec_att_W3': 8.0,
     'L0_rec_aug_Wr': 8.0,
     'L0_rec_aug_br': 8.0,
     'L0_rec_aug_Wu': 8.0,
     'L0_rec_aug_bu': 8.0,
     'L0_rec_aug_bh': 8.0,
     'L0_rec_dnn_b1': 64.0,
     'L0_rec_dnn_b2': 64.0}
    for name, (base, spread) in spreads.items():
        noise = np.random.default_rng([zlib.crc32(name.encode()), seed]).standard_normal(out[name].shape)
        drawn = base * np.exp(spread * noise) if base else spread * noise
        out[name] = jnp.asarray(drawn.astype(out[name].dtype))
    for name, factor in factors.items():
        out[name] = (out[name] * factor).astype(out[name].dtype)
    return out
```

```python
import concourse.bass as bass
from concourse import mybir
from contextlib import ExitStack


B = 512
P = 128
NC = B // P
T = 50
CANDS = 2500
USERS = 12500
H2 = 64
A = 32
G = P // A
LAG = 5
FIRST = LAG + 1
RING = 8
AHEAD = 4
LOOPS = (T - FIRST - AHEAD) // RING
EPS = 1e-5

(IH_R, IH_Z, IH_N, HH_R, HH_Z, HH_N, AUG_R, AUG_U, AUG_H, DNN_B1, BN1_G, BN1_B, ATT_B1, ATT_B2,
 DNN_B2, BN2_G, BN2_B, ATT_A1, ATT_A2, DNN_A1, DNN_A2, ATT_B3, DNN_B3, SMALL) = range(24)
(W_IR, W_IZ, W_IN, W_HR, W_HZ, W_HN, W_ARX, W_AUX, W_AHX, W_ARH, W_AUH, W_AHH,
 W_DU, W_DC, W_DH, WEIGHTS) = range(16)
SPLIT = W_AHX + 1


def recommender(nc, recent_idx, user_idx, cand_idx, user_emb, cand_emb, recent_emb,
                weights, small, att_w1, att_w2, att_w3, dnn_w2, dnn_w3, out):
    fp32 = mybir.dt.float32
    fp32r = mybir.dt.float32r
    i32 = mybir.dt.int32
    ALU = mybir.AluOpType
    ACT = mybir.ActivationFunctionType

    with ExitStack() as ctx:
        def sb(name, shape, dt=fp32):
            return ctx.enter_context(nc.sbuf_tensor(name, shape, dt))

        def sem(name):
            return ctx.enter_context(nc.semaphore(name))

        w = sb("w", [P, WEIGHTS, P])
        w_hi = sb("w_hi", [P, SPLIT, P], fp32r)
        w_lo = sb("w_lo", [P, SPLIT, P], fp32r)
        sm = sb("sm", [P, SMALL])
        bias_r = sb("bias_r", [P, 1])
        bias_z = sb("bias_z", [P, 1])
        w1 = sb("w1", [P, 4, A])
        w1_hs = sb("w1_hs", [P, A])
        w1_c = sb("w1_c", [P, G, A])
        w2_diag = sb("w2_diag", [P, P])
        w3_diag = sb("w3_diag", [P, G])
        d2 = sb("d2", [P, H2])
        d3 = sb("d3", [H2, 1])
        identity = sb("identity", [P, P])

        idx_raw = sb("idx_raw", [P, T + 2, NC], i32)
        idx_off = sb("idx_off", [P, T + 2, NC], i32)
        idx_neg = sb("idx_neg", [P, T + 2, NC])
        idx_flt = sb("idx_flt", [P, T + 2, NC])
        idx_all = sb("idx_all", [P, T + 2, NC], i32)
        idx_now = sb("idx_now", [P, AHEAD, NC], i32)
        fix_raw = sb("fix_raw", [P, 2, NC], i32)
        fix_neg = sb("fix_neg", [P, 2, NC])
        fix_flt = sb("fix_flt", [P, 2, NC])
        fix_idx = sb("fix_idx", [P, 2, NC], i32)

        rows = sb("rows", [P, RING, NC, P])
        fix_rows = sb("fix_rows", [P, 2, NC, P])
        x_hi = sb("x_hi", [P, 2, B], fp32r)
        x_lo = sb("x_lo", [P, 2, B], fp32r)
        user_t = sb("user_t", [P, B])
        cand_t = sb("cand_t", [P, B])

        h = sb("h", [P, RING, B])
        h_hi = sb("h_hi", [P, RING, B], fp32r)
        h_lo = sb("h_lo", [P, RING, B], fp32r)
        r = sb("r", [P, B])
        z = sb("z", [P, B])
        rhn = sb("rhn", [P, B])
        n_pre = sb("n_pre", [P, B])
        n = sb("n", [P, B])
        zh = sb("zh", [P, B])
        zn = sb("zn", [P, B])
        hc = sb("hc", [P, G, B])

        att_c = sb("att_c", [P, B])
        att_v1 = sb("att_v1", [P, B])
        att_n1 = sb("att_n1", [P, B])
        att_o1 = sb("att_o1", [P, B])
        att_v2 = sb("att_v2", [P, B])
        att_n2 = sb("att_n2", [P, B])
        att_o2 = sb("att_o2", [P, B])
        score = sb("score", [G, B])
        score_all = sb("score_all", [P, 2, G, B])
        score_dram = nc.dram_tensor("score_dram", [G, B], fp32, kind="Internal").ap()

        ah = sb("ah", [P, 2, B])
        ar = sb("ar", [P, B])
        au = sb("au", [P, B])
        su = sb("su", [P, B])
        rh = sb("rh", [P, B])
        hhat = sb("hhat", [P, B])
        keep = sb("keep", [P, B])
        take = sb("take", [P, B])

        dx = sb("dx", [P, B])
        dy = sb("dy", [P, B])
        dn = sb("dn", [P, B])
        dz1 = sb("dz1", [P, B])
        dz2 = sb("dz2", [H2, B])
        stats = sb("stats", [P, 6])
        aggr = sb("aggr", [P, 2])
        var_eps = sb("var_eps", [P, 1])
        std = sb("std", [P, 1])
        rstd = sb("rstd", [P, 1])
        gain = sb("gain", [P, 1])
        mgain = sb("mgain", [P, 1])
        shift = sb("shift", [P, 1])
        y = sb("y", [1, B])

        def bank(name):
            return ctx.enter_context(nc.psum_tensor(name, [P, B], fp32))

        ps_r, ps_z, ps_nx, ps_nh = bank("ps_r"), bank("ps_z"), bank("ps_nx"), bank("ps_nh")
        ps_ar, ps_au, ps_ah, ps_misc = bank("ps_ar"), bank("ps_au"), bank("ps_ah"), bank("ps_misc")

        idx_loaded, small_loaded, w_loaded, att_loaded, dnn_loaded = map(
            sem, ("idx_loaded", "small_loaded", "w_loaded", "att_loaded", "dnn_loaded"))
        diag_cleared, identity_step, offsets_made = map(sem, ("diag_cleared", "identity_step", "offsets_made"))
        idx_step, idx_ready, idx_copied = map(sem, ("idx_step", "idx_ready", "idx_copied"))
        gathered = [sem(f"gathered{s}") for s in range(RING)]
        fix_gathered = sem("fix_gathered")
        setup_step, w_ready, states_zeroed = map(sem, ("setup_step", "w_ready", "states_zeroed"))
        fix_turned, fix_copied, cand_done, att_c_ready = map(
            sem, ("fix_turned", "fix_copied", "cand_done", "att_c_ready"))
        x_turned, x_hi_ready, x_lo_ready = map(sem, ("x_turned", "x_hi_ready", "x_lo_ready"))
        nx_done, r_done, nh_done, z_done = map(sem, ("nx_done", "r_done", "nh_done", "z_done"))
        r_ready, z_ready, n_ready = map(sem, ("r_ready", "z_ready", "n_ready"))
        rhn_ready, n_pre_ready, zh_ready, zn_ready = map(sem, ("rhn_ready", "n_pre_ready", "zh_ready", "zn_ready"))
        h_ready, h_hi_ready, h_lo_ready, hc_ready = map(sem, ("h_ready", "h_hi_ready", "h_lo_ready", "hc_ready"))
        att1_done, att2_done, att3_done = map(sem, ("att1_done", "att2_done", "att3_done"))
        v1_ready, n1_ready, o1_ready, v2_ready, n2_ready, o2_ready = map(
            sem, ("v1_ready", "n1_ready", "o1_ready", "v2_ready", "n2_ready", "o2_ready"))
        score_ready, score_stored, score_spread = map(sem, ("score_ready", "score_stored", "score_spread"))
        ar_done, au_done, ah_done = map(sem, ("ar_done", "au_done", "ah_done"))
        ar_ready, au_ready, hhat_ready = map(sem, ("ar_ready", "au_ready", "hhat_ready"))
        rh_ready, su_ready, keep_ready, take_ready, ah_ready = map(
            sem, ("rh_ready", "su_ready", "keep_ready", "take_ready", "ah_ready"))
        dnn1_done, dnn2_done, dnn3_done, dnn_step, var_ready, std_ready, y_ready, stored = map(
            sem, ("dnn1_done", "dnn2_done", "dnn3_done", "dnn_step", "var_ready", "std_ready", "y_ready", "stored"))

        def col(c, parts=P):
            return sm[0:parts, c:c + 1]

        def exists(i, k):
            return 0 <= RING * i + k < T if isinstance(i, int) else True

        def count(eng, semaphore, value):
            if not isinstance(value, int) or value > 0:
                eng.wait_ge(semaphore, value)

        def ends_group(i, k):
            return exists(i, k) and (k % G == G - 1 or (isinstance(i, int) and RING * i + k == T - 1))

        def group(i, k):
            return (RING // G) * i + k // G

        def run(eng, step):
            for k in range(FIRST):
                step(0, k)
            with eng.Fori(0, LOOPS) as i:
                for k in range(FIRST, FIRST + RING):
                    step(i, k)
            for k in range(FIRST, T + LAG - RING * LOOPS):
                step(LOOPS, k)

        block = ctx.enter_context(nc.Block())

        @block.sync
        def _(sp):
            sp.dma_start(idx_raw[:, 0:T, :], recent_idx).then_inc(idx_loaded, 16)
            sp.dma_start(fix_raw[:, 0, :], user_idx).then_inc(idx_loaded, 16)
            sp.dma_start(fix_raw[:, 1, :], cand_idx).then_inc(idx_loaded, 16)
            sp.dma_start(w[:, 0:SPLIT, :], weights[:, 0:SPLIT, :]).then_inc(w_loaded, 16)
            sp.dma_start(sm[:], small).then_inc(small_loaded, 16)
            sp.dma_start(w[:, SPLIT:WEIGHTS, :], weights[:, SPLIT:WEIGHTS, :]).then_inc(w_loaded, 16)
            sp.dma_start(w1[:], att_w1).then_inc(att_loaded, 16)
            sp.dma_start(d2[:], dnn_w2).then_inc(dnn_loaded, 16)
            sp.dma_start(d3[:], dnn_w3).then_inc(dnn_loaded, 16)
            sp.wait_ge(diag_cleared, 2)
            for j in range(G):
                block_j = slice(A * j, A * (j + 1))
                sp.dma_start(w2_diag[block_j, block_j], att_w2).then_inc(att_loaded, 16)
                sp.dma_start(w3_diag[block_j, j:j + 1], att_w3).then_inc(att_loaded, 16)

            for g in range(-(-T // G)):
                sp.wait_ge(score_ready, g + 1)
                count(sp, score_spread, 16 * g)
                sp.dma_start(score_dram, score[:]).then_inc(score_stored, 16)
                sp.wait_ge(score_stored, 16 * g + 16)
                count(sp, su_ready, G * g - G)
                sp.dma_start(score_all[:, g % 2, :, :],
                             score_dram.unsqueeze(0).broadcast_to([P, G, B])).then_inc(score_spread, 16)
            sp.wait_ge(y_ready, 1)
            sp.dma_start(out, y[:]).then_inc(stored, 16)
            sp.wait_ge(stored, 16)

        @block.gpsimd
        def _(pool):
            nc.gpsimd.iota(idx_off[:], pattern=[[CANDS, T + 2], [0, NC]], base=0,
                           channel_multiplier=0).then_inc(offsets_made, 1)
            nc.gpsimd.memset(identity[:], 0.0).then_inc(identity_step, 1)
            pool.wait_ge(identity_step, 1)
            nc.gpsimd.affine_select(out=identity[:], in_=identity[:], compare_op=ALU.not_equal, fill=1.0,
                                    base=0, pattern=[[-1, P]], channel_multiplier=1).then_inc(identity_step, 1)

            def place_indices(i, k):
                if not (isinstance(i, int) and RING * i + k == 0):
                    pool.wait_ge(gathered[(k - 1) % RING], 16 * NC * (i + (k - 1) // RING + 1))
                nc.gpsimd.tensor_copy(idx_now[:], idx_all[:, bass.ds(RING * i + k, AHEAD), :])\
                    .then_inc(idx_copied, 1)
                pool.wait_ge(idx_copied, (RING // AHEAD) * i + k // AHEAD + 1)

            def gather(i, k):
                for c in range(NC):
                    nc.gpsimd.indirect_dma_start(
                        rows[:, k % RING, c, :], None, recent_emb,
                        bass.IndirectOffsetOnAxis(ap=idx_now[:, k % AHEAD, c:c + 1], axis=0))\
                        .then_inc(gathered[k % RING], 16)

            pool.wait_ge(idx_ready, 1)
            place_indices(0, 0)
            gather(0, 0)
            for f, table in enumerate((user_emb, cand_emb)):
                for c in range(NC):
                    nc.gpsimd.indirect_dma_start(
                        fix_rows[:, f, c, :], None, table,
                        bass.IndirectOffsetOnAxis(ap=fix_idx[:, f, c:c + 1], axis=0)).then_inc(fix_gathered, 16)
            for k in range(1, AHEAD):
                gather(0, k)
            place_indices(0, AHEAD)

            def step(i, k):
                t = RING * i + k
                if exists(i, k + AHEAD):
                    gather(i, k + AHEAD)
                if exists(i, k):
                    pool.wait_ge(z_ready, t + 1)
                    count(pool, h_ready, t)
                    nc.gpsimd.tensor_tensor(zh[:], z[:], h[:, (k - 1) % RING, :], ALU.mult).then_inc(zh_ready, 1)
                if exists(i, k - LAG):
                    s = t - LAG
                    pool.wait_ge(score_spread, 16 * group(i, k - LAG) + 16)
                    pool.wait_ge(au_ready, s + 1)
                    nc.gpsimd.tensor_tensor(su[:], au[:], score_all[:, ((k - LAG) // G) % 2, (k - LAG) % G, :],
                                            ALU.mult).then_inc(su_ready, 1)
                if (k + 1) % AHEAD == 0 and exists(i, k + 1 + AHEAD):
                    place_indices(i, k + 1 + AHEAD)
                if exists(i, k):
                    pool.wait_ge(h_ready, t + 1)
                    nc.gpsimd.tensor_tensor(hc[:, k % G, :], h[:, k % RING, :], cand_t[:], ALU.mult)\
                        .then_inc(hc_ready, 1)

            pool.wait_ge(fix_copied, 2)
            pool.wait_ge(states_zeroed, 4)
            run(pool, step)

        @block.scalar
        def _(act):
            def split_x(i, k):
                act.wait_ge(x_turned, RING * i + k + 1)
                nc.scalar.activation(x_hi[:, k % 2, :], ps_misc[:], ACT.Copy).then_inc(x_hi_ready, 1)

            for f, dst in enumerate((user_t, cand_t)):
                act.wait_ge(fix_turned, f + 1)
                nc.scalar.activation(dst[:], ps_misc[:], ACT.Copy).then_inc(fix_copied, 1)
            split_x(0, 0)
            split_x(0, 1)

            def step(i, k):
                t = RING * i + k
                gru, aug = exists(i, k), exists(i, k - LAG)
                if gru:
                    act.wait_ge(r_done, t + 1)
                    nc.scalar.activation(r[:], ps_r[:], ACT.Sigmoid, bias=bias_r[:]).then_inc(r_ready, 1)
                    act.wait_ge(z_done, t + 1)
                    nc.scalar.activation(z[:], ps_z[:], ACT.Sigmoid, bias=bias_z[:]).then_inc(z_ready, 1)
                if aug:
                    s = t - LAG
                    act.wait_ge(ar_done, s + 1)
                    nc.scalar.activation(ar[:], ps_ar[:], ACT.Sigmoid, bias=col(AUG_R)).then_inc(ar_ready, 1)
                if gru:
                    act.wait_ge(n_pre_ready, t + 1)
                    nc.scalar.activation(n[:], n_pre[:], ACT.Tanh, bias=col(IH_N)).then_inc(n_ready, 1)
                if ends_group(i, k - 1):
                    g = group(i, k - 1)
                    act.wait_ge(att2_done, g + 1)
                    nc.scalar.activation(att_v2[:], ps_misc[:], ACT.Identity, bias=col(ATT_B2)).then_inc(v2_ready, 1)
                if aug:
                    act.wait_ge(au_done, s + 1)
                    nc.scalar.activation(au[:], ps_au[:], ACT.Sigmoid, bias=col(AUG_U)).then_inc(au_ready, 1)
                if exists(i, k + 2):
                    split_x(i, k + 2)
                if aug:
                    act.wait_ge(ah_done, s + 1)
                    nc.scalar.activation(hhat[:], ps_ah[:], ACT.Tanh, bias=col(AUG_H)).then_inc(hhat_ready, 1)
                if ends_group(i, k - 1):
                    act.wait_ge(att3_done, g + 1)
                    count(act, score_stored, 16 * g)
                    nc.scalar.activation(score[:], ps_misc[0:G, :], ACT.Sigmoid, bias=col(ATT_B3, G))\
                        .then_inc(score_ready, 1)

            run(act, step)
            for layer, parts in ((0, P), (1, H2)):
                act.wait_ge(var_ready, layer + 1)
                nc.scalar.activation(std[0:parts], var_eps[0:parts], ACT.Sqrt).then_inc(std_ready, 1)

        @block.vector
        def _(dve):
            nc.vector.memset(w2_diag[:], 0.0).then_inc(diag_cleared, 1)
            nc.vector.memset(w3_diag[:], 0.0).then_inc(diag_cleared, 1)
            for state in (h, h_hi, h_lo):
                last = state[:, RING - 1, :]
                nc.vector.memset(last.bitcast(fp32) if state is not h else last, 0.0).then_inc(states_zeroed, 1)
            nc.vector.memset(ah[:, 1, :], 0.0).then_inc(states_zeroed, 1)
            nc.vector.memset(idx_all[:], 0).then_inc(idx_step, 1)

            dve.wait_ge(idx_loaded, 48)
            steps = 1

            def idx_op(ins):
                nonlocal steps
                steps += 1
                ins.then_inc(idx_step, 1)
                dve.wait_ge(idx_step, steps)

            idx_op(nc.vector.tensor_scalar(idx_neg[:, 0:T, :], idx_raw[:, 0:T, :], 0.0, float(CANDS), ALU.is_lt, ALU.mult))
            idx_op(nc.vector.tensor_tensor(idx_flt[:, 0:T, :], idx_raw[:, 0:T, :], idx_neg[:, 0:T, :], ALU.add))
            idx_op(nc.vector.tensor_scalar(idx_flt[:, 0:T, :], idx_flt[:, 0:T, :], 0.0, float(CANDS - 1), ALU.max, ALU.min))
            for f, size in enumerate((USERS, CANDS)):
                idx_op(nc.vector.tensor_scalar(fix_neg[:, f, :], fix_raw[:, f, :], 0.0, float(size), ALU.is_lt, ALU.mult))
                idx_op(nc.vector.tensor_tensor(fix_flt[:, f, :], fix_raw[:, f, :], fix_neg[:, f, :], ALU.add))
                idx_op(nc.vector.tensor_scalar(fix_idx[:, f, :], fix_flt[:, f, :], 0.0, float(size - 1), ALU.max, ALU.min))
            dve.wait_ge(offsets_made, 1)
            nc.vector.tensor_tensor(idx_all[:, 0:T, :], idx_flt[:, 0:T, :], idx_off[:, 0:T, :], ALU.add)\
                .then_inc(idx_ready, 1)

            dve.wait_ge(w_loaded, 32)
            nc.vector.tensor_copy(w_hi[:], w[:, 0:SPLIT, :]).then_inc(setup_step, 1)
            dve.wait_ge(setup_step, 1)
            nc.vector.tensor_tensor(w_lo[:], w[:, 0:SPLIT, :], w_hi[:].bitcast(fp32), ALU.subtract).then_inc(w_ready, 1)
            dve.wait_ge(small_loaded, 16)
            nc.vector.tensor_tensor(bias_r[:], col(IH_R), col(HH_R), ALU.add).then_inc(w_ready, 1)
            nc.vector.tensor_tensor(bias_z[:], col(IH_Z), col(HH_Z), ALU.add).then_inc(w_ready, 1)
            dve.wait_ge(att_loaded, 16 * (1 + 2 * G))
            nc.vector.tensor_tensor(w1_hs[:], w1[:, 0, :], w1[:, 2, :], ALU.add).then_inc(w_ready, 1)
            for j in range(G):
                nc.vector.tensor_tensor(w1_c[:, j, :], w1[:, 1, :], w1[:, 2, :], ALU.subtract).then_inc(w_ready, 1)
            dve.wait_ge(cand_done, 1)
            nc.vector.tensor_scalar(att_c[:], ps_misc[:], col(ATT_B1), None, ALU.add).then_inc(att_c_ready, 1)

            def split_x(i, k):
                dve.wait_ge(x_hi_ready, RING * i + k + 1)
                nc.vector.tensor_tensor(x_lo[:, k % 2, :], ps_misc[:], x_hi[:, k % 2, :].bitcast(fp32),
                                        ALU.subtract).then_inc(x_lo_ready, 1)

            split_x(0, 0)
            split_x(0, 1)

            def step(i, k):
                t = RING * i + k
                gru, aug = exists(i, k), exists(i, k - LAG)
                slot = k % RING
                if ends_group(i, k - 1):
                    g = group(i, k - 1)
                    dve.wait_ge(att1_done, g + 1)
                    nc.vector.tensor_tensor(att_v1[:], ps_misc[:], att_c[:], ALU.add).then_inc(v1_ready, 1)
                    dve.wait_ge(v1_ready, g + 1)
                    nc.vector.tensor_scalar(att_n1[:], att_v1[:], 0.0, col(ATT_A1), ALU.min, ALU.mult).then_inc(n1_ready, 1)
                    dve.wait_ge(n1_ready, g + 1)
                    nc.vector.scalar_tensor_tensor(out=att_o1[:], in0=att_v1[:], scalar=0.0, in1=att_n1[:],
                                                   op0=ALU.max, op1=ALU.add).then_inc(o1_ready, 1)
                if gru:
                    dve.wait_ge(nh_done, t + 1)
                    dve.wait_ge(r_ready, t + 1)
                    nc.vector.scalar_tensor_tensor(out=rhn[:], in0=ps_nh[:], scalar=col(HH_N), in1=r[:],
                                                   op0=ALU.add, op1=ALU.mult).then_inc(rhn_ready, 1)
                    dve.wait_ge(nx_done, t + 1)
                    dve.wait_ge(rhn_ready, t + 1)
                    nc.vector.tensor_tensor(n_pre[:], ps_nx[:], rhn[:], ALU.add).then_inc(n_pre_ready, 1)
                if aug:
                    s = t - LAG
                    old = ah[:, (k - LAG - 1) % 2, :]
                    dve.wait_ge(ar_ready, s + 1)
                    count(dve, ah_ready, s)
                    nc.vector.tensor_tensor(rh[:], ar[:], old, ALU.mult).then_inc(rh_ready, 1)
                if gru:
                    dve.wait_ge(n_ready, t + 1)
                    nc.vector.scalar_tensor_tensor(out=zn[:], in0=z[:], scalar=1.0, in1=n[:],
                                                   op0=ALU.subtract, op1=ALU.mult).then_inc(zn_ready, 1)
                    dve.wait_ge(zh_ready, t + 1)
                    dve.wait_ge(zn_ready, t + 1)
                    nc.vector.tensor_tensor(h[:, slot, :], zh[:], zn[:], ALU.subtract).then_inc(h_ready, 1)
                    dve.wait_ge(h_ready, t + 1)
                    nc.vector.tensor_copy(h_hi[:, slot, :], h[:, slot, :]).then_inc(h_hi_ready, 1)
                    dve.wait_ge(h_hi_ready, t + 1)
                    nc.vector.tensor_tensor(h_lo[:, slot, :], h[:, slot, :], h_hi[:, slot, :].bitcast(fp32),
                                            ALU.subtract).then_inc(h_lo_ready, 1)
                if ends_group(i, k - 1):
                    dve.wait_ge(v2_ready, g + 1)
                    nc.vector.tensor_scalar(att_n2[:], att_v2[:], 0.0, col(ATT_A2), ALU.min, ALU.mult).then_inc(n2_ready, 1)
                    dve.wait_ge(n2_ready, g + 1)
                    nc.vector.scalar_tensor_tensor(out=att_o2[:], in0=att_v2[:], scalar=0.0, in1=att_n2[:],
                                                   op0=ALU.max, op1=ALU.add).then_inc(o2_ready, 1)
                if exists(i, k + 2):
                    split_x(i, k + 2)
                if aug:
                    dve.wait_ge(su_ready, s + 1)
                    nc.vector.scalar_tensor_tensor(out=keep[:], in0=su[:], scalar=1.0, in1=old,
                                                   op0=ALU.subtract, op1=ALU.mult).then_inc(keep_ready, 1)
                    dve.wait_ge(hhat_ready, s + 1)
                    nc.vector.tensor_tensor(take[:], su[:], hhat[:], ALU.mult).then_inc(take_ready, 1)
                    dve.wait_ge(keep_ready, s + 1)
                    dve.wait_ge(take_ready, s + 1)
                    nc.vector.tensor_tensor(ah[:, (k - LAG) % 2, :], take[:], keep[:], ALU.subtract).then_inc(ah_ready, 1)

            run(dve, step)

            done = 0

            def link(ins):
                nonlocal done
                done += 1
                ins.then_inc(dnn_step, 1)
                dve.wait_ge(dnn_step, done)

            for layer, (parts, ps, made, b, g_, b_, a, dst) in enumerate((
                    (P, ps_r, dnn1_done, DNN_B1, BN1_G, BN1_B, DNN_A1, dz1),
                    (H2, ps_z, dnn2_done, DNN_B2, BN2_G, BN2_B, DNN_A2, dz2))):
                on = slice(0, parts)
                dve.wait_ge(made, 1)
                link(nc.vector.tensor_scalar(dx[on], ps[on], col(b, parts), None, ALU.add))
                link(nc.vector.bn_stats(stats[on], dx[on]))
                link(nc.vector.bn_aggr(aggr[on], stats[on]))
                nc.vector.tensor_scalar(var_eps[on], aggr[on, 1:2], EPS, None, ALU.add).then_inc(var_ready, 1)
                dve.wait_ge(std_ready, layer + 1)
                link(nc.vector.reciprocal(rstd[on], std[on]))
                link(nc.vector.tensor_tensor(gain[on], rstd[on], col(g_, parts), ALU.mult))
                link(nc.vector.tensor_tensor(mgain[on], aggr[on, 0:1], gain[on], ALU.mult))
                link(nc.vector.tensor_tensor(shift[on], col(b_, parts), mgain[on], ALU.subtract))
                link(nc.vector.tensor_scalar(dy[on], dx[on], gain[on], shift[on], ALU.mult, ALU.add))
                link(nc.vector.tensor_scalar(dn[on], dy[on], 0.0, col(a, parts), ALU.min, ALU.mult))
                link(nc.vector.scalar_tensor_tensor(out=dst[on], in0=dy[on], scalar=0.0, in1=dn[on],
                                                    op0=ALU.max, op1=ALU.add))
            dve.wait_ge(dnn3_done, 1)
            nc.vector.tensor_scalar(y[:], ps_nx[0:1, :], col(DNN_B3, 1), None, ALU.add).then_inc(y_ready, 1)

        @block.tensor
        def _(pe):
            mm = nc.tensor.matmul

            def turn(src, semaphore):
                for c in range(NC):
                    last = nc.tensor.transpose(ps_misc[:, c * P:(c + 1) * P], src[:, c, :], identity[:])
                last.then_inc(semaphore, 1)

            def turn_x(i, k):
                pe.wait_ge(gathered[k % RING], 16 * NC * (i + k // RING + 1))
                turn(rows[:, k % RING], x_turned)

            def exact(ps, block_, hi, lo, start, stop):
                mm(ps[:], w_hi[:, block_, :], hi, start=start, stop=False)
                mm(ps[:], w_lo[:, block_, :], hi, start=False, stop=False)
                return mm(ps[:], w_hi[:, block_, :], lo, start=False, stop=stop)

            def input_gates(i, k):
                t = RING * i + k
                pe.wait_ge(x_hi_ready, t + 1)
                pe.wait_ge(x_lo_ready, t + 1)
                hi, lo = x_hi[:, k % 2, :], x_lo[:, k % 2, :]
                count(pe, r_ready, t)
                exact(ps_r, W_IR, hi, lo, True, False)
                count(pe, n_pre_ready, t)
                exact(ps_nx, W_IN, hi, lo, True, True).then_inc(nx_done, 1)
                count(pe, z_ready, t)
                exact(ps_z, W_IZ, hi, lo, True, False)

            pe.wait_ge(identity_step, 2)
            pe.wait_ge(fix_gathered, 16 * 2 * NC)
            turn(fix_rows[:, 0], fix_turned)
            pe.wait_ge(fix_copied, 1)
            turn(fix_rows[:, 1], fix_turned)
            pe.wait_ge(fix_copied, 2)
            pe.wait_ge(w_ready, 4 + G)
            mm(ps_misc[:], w1_c[:].rearrange("p g a -> p (g a)"), cand_t[:], start=True, stop=True).then_inc(cand_done, 1)
            pe.wait_ge(att_c_ready, 1)
            turn_x(0, 0)
            pe.wait_ge(x_lo_ready, 1)
            turn_x(0, 1)
            input_gates(0, 0)
            pe.wait_ge(states_zeroed, 4)

            def step(i, k):
                t = RING * i + k
                gru, aug = exists(i, k), exists(i, k - LAG)
                prev = (k - 1) % RING
                if gru:
                    hi, lo = h_hi[:, prev, :], h_lo[:, prev, :]
                    count(pe, h_hi_ready, t)
                    mm(ps_r[:], w_hi[:, W_HR, :], hi, start=False, stop=False)
                    mm(ps_r[:], w_lo[:, W_HR, :], hi, start=False, stop=False)
                    count(pe, rhn_ready, t)
                    mm(ps_nh[:], w_hi[:, W_HN, :], hi, start=True, stop=False)
                    mm(ps_nh[:], w_lo[:, W_HN, :], hi, start=False, stop=False)
                    count(pe, h_lo_ready, t)
                    mm(ps_r[:], w_hi[:, W_HR, :], lo, start=False, stop=True).then_inc(r_done, 1)
                    mm(ps_nh[:], w_hi[:, W_HN, :], lo, start=False, stop=True).then_inc(nh_done, 1)
                    exact(ps_z, W_HZ, hi, lo, False, True).then_inc(z_done, 1)
                if aug:
                    s = t - LAG
                    old = ah[:, (k - LAG - 1) % 2, :]
                    count(pe, ah_ready, s)
                    mm(ps_ar[:], w[:, W_ARH, :], old, start=False, stop=True).then_inc(ar_done, 1)
                if ends_group(i, k - 1):
                    g = group(i, k - 1)
                    pe.wait_ge(o1_ready, g + 1)
                    mm(ps_misc[:], w2_diag[:], att_o1[:], start=True, stop=True).then_inc(att2_done, 1)
                if aug:
                    mm(ps_au[:], w[:, W_AUH, :], old, start=False, stop=True).then_inc(au_done, 1)
                if exists(i, k + 2):
                    if ends_group(i, k - 1):
                        pe.wait_ge(v2_ready, g + 1)
                    elif ends_group(i, k - 2):
                        pe.wait_ge(score_ready, group(i, k - 2) + 1)
                    else:
                        pe.wait_ge(x_lo_ready, t + 2)
                    turn_x(i, k + 2)
                if exists(i, k + 1):
                    input_gates(i, k + 1)
                if aug:
                    slot = (k - LAG) % RING
                    count(pe, hhat_ready, s)
                    exact(ps_ah, W_AHX, h_hi[:, slot, :], h_lo[:, slot, :], True, False)
                    pe.wait_ge(rh_ready, s + 1)
                    mm(ps_ah[:], w[:, W_AHH, :], rh[:], start=False, stop=True).then_inc(ah_done, 1)
                if exists(i, k - LAG + 1):
                    slot = (k - LAG + 1) % RING
                    count(pe, ar_ready, t - LAG + 1)
                    exact(ps_ar, W_ARX, h_hi[:, slot, :], h_lo[:, slot, :], True, False)
                    count(pe, au_ready, t - LAG + 1)
                    exact(ps_au, W_AUX, h_hi[:, slot, :], h_lo[:, slot, :], True, False)
                if ends_group(i, k - 1):
                    if exists(i, k + 2):
                        pe.wait_ge(x_lo_ready, t + 3)
                    pe.wait_ge(o2_ready, g + 1)
                    mm(ps_misc[0:G, :], w3_diag[:], att_o2[:], start=True, stop=True).then_inc(att3_done, 1)
                if ends_group(i, k):
                    if exists(i, k + 2):
                        pe.wait_ge(x_lo_ready, t + 3)
                    first = k - k % G
                    pe.wait_ge(hc_ready, t + 1)
                    for j in range(G):
                        mm(ps_misc[A * j:A * (j + 1), :], w1_hs[:], h[:, (first + j) % RING, :], start=True, stop=False)
                    for j in range(G):
                        last = mm(ps_misc[A * j:A * (j + 1), :], w1[:, 3, :], hc[:, j, :], start=False, stop=True)
                    last.then_inc(att1_done, 1)

            run(pe, step)
            pe.wait_ge(w_loaded, 32)
            mm(ps_r[:], w[:, W_DU, :], user_t[:], start=True, stop=False)
            mm(ps_r[:], w[:, W_DC, :], cand_t[:], start=False, stop=False)
            pe.wait_ge(ah_ready, T)
            mm(ps_r[:], w[:, W_DH, :], ah[:, (T - 1) % 2, :], start=False, stop=True).then_inc(dnn1_done, 1)
            pe.wait_ge(dnn_loaded, 32)
            pe.wait_ge(dnn_step, 10)
            mm(ps_z[0:H2, :], d2[:], dz1[:], start=True, stop=True).then_inc(dnn2_done, 1)
            pe.wait_ge(dnn_step, 20)
            mm(ps_nx[0:1, :], d3[:], dz2[:], start=True, stop=True).then_inc(dnn3_done, 1)


def kernel(**inputs):
    import numpy as np
    import concourse.bacc as bacc
    from concourse.bass_utils import run_bass_kernel_spmd

    x = {name.replace("L0_rec_", ""): np.asarray(a) for name, a in inputs.items()}

    def rows_of(a, n):
        return a.reshape(n, P, a.shape[1]).transpose(1, 0, 2)

    def chunks(idx):
        return np.ascontiguousarray(idx.reshape(NC, P, -1).transpose(1, 2, 0))

    ih, hh = rows_of(x["gru_W_ih"], 3), rows_of(x["gru_W_hh"], 3)
    wr, wu, wh = (rows_of(x[k], 2) for k in ("aug_Wr", "aug_Wu", "aug_Wh"))
    dnn = rows_of(x["dnn_W1"], 3)
    weights = np.empty((P, WEIGHTS, P), np.float32)
    for block, a in ((W_IR, ih[:, 0].T), (W_IZ, ih[:, 1].T), (W_IN, ih[:, 2].T),
                     (W_HR, hh[:, 0].T), (W_HZ, hh[:, 1].T), (W_HN, hh[:, 2].T),
                     (W_ARX, wr[:, 0]), (W_ARH, wr[:, 1]), (W_AUX, wu[:, 0]), (W_AUH, wu[:, 1]),
                     (W_AHH, wh[:, 0]), (W_AHX, wh[:, 1]), (W_DU, dnn[:, 0]), (W_DC, dnn[:, 1]), (W_DH, dnn[:, 2])):
        weights[:, block] = a
    small = np.zeros((P, SMALL), np.float32)
    for c, a in ((IH_R, x["gru_b_ih"][0:P]), (IH_Z, x["gru_b_ih"][P:2 * P]), (IH_N, x["gru_b_ih"][2 * P:]),
                 (HH_R, x["gru_b_hh"][0:P]), (HH_Z, x["gru_b_hh"][P:2 * P]), (HH_N, x["gru_b_hh"][2 * P:]),
                 (AUG_R, x["aug_br"]), (AUG_U, x["aug_bu"]), (AUG_H, x["aug_bh"]),
                 (DNN_B1, x["dnn_b1"]), (BN1_G, x["bn1_g"]), (BN1_B, x["bn1_b"]),
                 (ATT_B1, np.tile(x["att_b1"], G)), (ATT_B2, np.tile(x["att_b2"], G)),
                 (DNN_B2, x["dnn_b2"]), (BN2_G, x["bn2_g"]), (BN2_B, x["bn2_b"])):
        small[0:a.shape[0], c] = a
    for c, name in ((ATT_A1, "att_a1"), (ATT_A2, "att_a2"), (DNN_A1, "dnn_a1"), (DNN_A2, "dnn_a2"),
                    (ATT_B3, "att_b3"), (DNN_B3, "dnn_b3")):
        small[:, c] = x[name].reshape(())
    arrays = {
        "recent_idx": chunks(x["r_recent_features"]),
        "user_idx": chunks(x["r_user_features"])[:, 0],
        "cand_idx": chunks(x["r_candidate_features"])[:, 0],
        "user_emb": x["user_emb"],
        "cand_emb": x["cand_emb"],
        "recent_emb": x["recent_emb"].reshape(T * CANDS, P),
        "weights": weights,
        "small": small,
        "att_w1": rows_of(x["att_W1"], 4),
        "att_w2": x["att_W2"],
        "att_w3": x["att_W3"],
        "dnn_w2": x["dnn_W2"],
        "dnn_w3": x["dnn_W3"],
    }
    arrays = {name: np.ascontiguousarray(a) for name, a in arrays.items()}

    nc = bacc.Bacc("TRN2", target_bir_lowering=False, num_devices=1)
    aps = {name: nc.dram_tensor(name, a.shape, mybir.dt.from_np(a.dtype), kind="ExternalInput").ap()
           for name, a in arrays.items()}
    out = nc.dram_tensor("out", (1, B), mybir.dt.float32, kind="ExternalOutput").ap()
    recommender(nc, **aps, out=out)
    result = run_bass_kernel_spmd(nc, [arrays], core_ids=[0])
    return result.results[0]["out"].reshape(B, 1)
```

```python
import concourse.bass as bass
from concourse import mybir
from contextlib import ExitStack


B = 512
P = 128
NC = B // P
T = 50
CANDS = 2500
USERS = 12500
H2 = 64
A = 32
G = P // A
LAG = 5
FIRST = LAG + 1
RING = 8
AHEAD = 4
LOOPS = (T - FIRST - AHEAD) // RING
EPS = 1e-5

(IH_R, IH_Z, IH_N, HH_R, HH_Z, HH_N, AUG_R, AUG_U, AUG_H, DNN_B1, BN1_G, BN1_B, ATT_B1, ATT_B2,
 DNN_B2, BN2_G, BN2_B, ATT_A1, ATT_A2, DNN_A1, DNN_A2, ATT_B3, DNN_B3, SMALL) = range(24)
(W_IR, W_IZ, W_IN, W_HR, W_HZ, W_HN, W_ARX, W_AUX, W_AHX, W_ARH, W_AUH, W_AHH,
 W_DU, W_DC, W_DH, WEIGHTS) = range(16)
SPLIT = W_AUH + 1
INPUT = W_IN + 1


def recommender(nc, recent_idx, user_idx, cand_idx, user_emb, cand_emb, recent_emb,
                weights, small, att_w1, att_w2, att_w3, dnn_w2, dnn_w3, out):
    fp32 = mybir.dt.float32
    fp32r = mybir.dt.float32r
    i32 = mybir.dt.int32
    ALU = mybir.AluOpType
    ACT = mybir.ActivationFunctionType

    with ExitStack() as ctx:
        def sb(name, shape, dt=fp32):
            return ctx.enter_context(nc.sbuf_tensor(name, shape, dt))

        def sem(name):
            return ctx.enter_context(nc.semaphore(name))

        w = sb("w", [P, WEIGHTS, P])
        w_hi = sb("w_hi", [P, SPLIT, P], fp32r)
        w_lo = sb("w_lo", [P, SPLIT, P], fp32r)
        sm = sb("sm", [P, SMALL])
        bias_r = sb("bias_r", [P, 1])
        bias_z = sb("bias_z", [P, 1])
        att_nb2 = sb("att_nb2", [P, 1])
        att_na2 = sb("att_na2", [P, 1])
        w1 = sb("w1", [P, 4, A])
        w1_hs = sb("w1_hs", [P, A])
        w1_c = sb("w1_c", [P, G, A])
        w2_diag = sb("w2_diag", [P, P])
        w3_diag = sb("w3_diag", [P, G])
        d2 = sb("d2", [P, H2])
        d3 = sb("d3", [H2, 1])
        identity = sb("identity", [P, P])

        idx_raw = sb("idx_raw", [P, T + 2, NC], i32)
        idx_off = sb("idx_off", [P, T + 2, NC], i32)
        idx_neg = sb("idx_neg", [P, T + 2, NC])
        idx_flt = sb("idx_flt", [P, T + 2, NC])
        idx_all = sb("idx_all", [P, T + 2, NC], i32)
        idx_now = sb("idx_now", [P, 2, AHEAD, NC], i32)
        fix_raw = sb("fix_raw", [P, 2, NC], i32)
        fix_neg = sb("fix_neg", [P, 2, NC])
        fix_flt = sb("fix_flt", [P, 2, NC])
        fix_idx = sb("fix_idx", [P, 2, NC], i32)

        rows = sb("rows", [P, RING, NC, P])
        fix_rows = sb("fix_rows", [P, 2, NC, P])
        x_hi = sb("x_hi", [P, 2, B], fp32r)
        x_lo = sb("x_lo", [P, 2, B], fp32r)
        user_t = sb("user_t", [P, B])
        cand_t = sb("cand_t", [P, B])

        h = sb("h", [P, RING, B])
        h_hi = sb("h_hi", [P, RING, B], fp32r)
        h_lo = sb("h_lo", [P, RING, B], fp32r)
        r = sb("r", [P, B])
        z = sb("z", [P, B])
        rhn = sb("rhn", [P, B])
        n_pre = sb("n_pre", [P, B])
        n = sb("n", [P, B])
        zh = sb("zh", [P, B])
        zn = sb("zn", [P, B])
        hc = sb("hc", [P, G, B])

        att_c = sb("att_c", [P, B])
        att_v1 = sb("att_v1", [P, B])
        att_n1 = sb("att_n1", [P, B])
        att_o1 = sb("att_o1", [P, B])
        att_p2 = sb("att_p2", [P, B])
        att_n2 = sb("att_n2", [P, B])
        att_o2 = sb("att_o2", [P, B])
        score = sb("score", [G, B])
        score_all = sb("score_all", [P, 2, G, B])
        score_dram = nc.dram_tensor("score_dram", [G, B], fp32, kind="Internal").ap()

        ah = sb("ah", [P, 2, B])
        ah_hi = sb("ah_hi", [P, B], fp32r)
        ah_lo = sb("ah_lo", [P, B], fp32r)
        ar = sb("ar", [P, B])
        au = sb("au", [P, B])
        su = sb("su", [P, B])
        rh = sb("rh", [P, B])
        hhat = sb("hhat", [P, B])
        keep = sb("keep", [P, B])
        take = sb("take", [P, B])

        dx = sb("dx", [P, B])
        dy = sb("dy", [P, B])
        dn = sb("dn", [P, B])
        dz1 = sb("dz1", [P, B])
        dz2 = sb("dz2", [H2, B])
        stats = sb("stats", [P, 6])
        aggr = sb("aggr", [P, 2])
        var_eps = sb("var_eps", [P, 1])
        std = sb("std", [P, 1])
        rstd = sb("rstd", [P, 1])
        gain = sb("gain", [P, 1])
        mgain = sb("mgain", [P, 1])
        shift = sb("shift", [P, 1])
        y = sb("y", [1, B])

        def bank(name):
            return ctx.enter_context(nc.psum_tensor(name, [P, B], fp32))

        ps_r, ps_z, ps_nx, ps_nh = bank("ps_r"), bank("ps_z"), bank("ps_nx"), bank("ps_nh")
        ps_x, ps_att, ps_au = bank("ps_x"), bank("ps_att"), bank("ps_au")
        ps_a = bank("ps_a")

        fix_idx_loaded, input_w_loaded, rest_w_loaded = map(
            sem, ("fix_idx_loaded", "input_w_loaded", "rest_w_loaded"))
        idx_loaded, small_loaded, w_loaded, att_loaded, dnn_loaded = map(
            sem, ("idx_loaded", "small_loaded", "w_loaded", "att_loaded", "dnn_loaded"))
        diag_cleared, identity_step, offsets_made = map(sem, ("diag_cleared", "identity_step", "offsets_made"))
        idx_step, idx_ready, idx_copied = map(sem, ("idx_step", "idx_ready", "idx_copied"))
        gathered = [sem(f"gathered{s}") for s in range(RING)]
        fix_gathered = [sem("user_gathered"), sem("cand_gathered")]
        setup_step, w_ready, bias_ready, states_zeroed = map(
            sem, ("setup_step", "w_ready", "bias_ready", "states_zeroed"))
        fix_turned, fix_copied, cand_done, att_c_ready, att_w_ready = map(
            sem, ("fix_turned", "fix_copied", "cand_done", "att_c_ready", "att_w_ready"))
        x_turned, x_hi_ready, x_lo_ready = map(sem, ("x_turned", "x_hi_ready", "x_lo_ready"))
        nx_done, r_done, nh_done, z_done = map(sem, ("nx_done", "r_done", "nh_done", "z_done"))
        r_ready, z_ready, n_ready = map(sem, ("r_ready", "z_ready", "n_ready"))
        rhn_ready, n_pre_ready, zh_ready, zn_ready = map(sem, ("rhn_ready", "n_pre_ready", "zh_ready", "zn_ready"))
        h_ready, h_hi_ready, h_lo_ready, hc_ready = map(sem, ("h_ready", "h_hi_ready", "h_lo_ready", "hc_ready"))
        att1_done, att2_done, att3_done = map(sem, ("att1_done", "att2_done", "att3_done"))
        v1_ready, n1_ready, o1_ready, p2_ready, n2_ready, o2_ready = map(
            sem, ("v1_ready", "n1_ready", "o1_ready", "p2_ready", "n2_ready", "o2_ready"))
        score_ready, score_stored = map(sem, ("score_ready", "score_stored"))
        spread = [sem(f"spread{j}") for j in range(G)]
        ar_done, au_done, ah_done = map(sem, ("ar_done", "au_done", "ah_done"))
        ar_ready, au_ready, hhat_ready = map(sem, ("ar_ready", "au_ready", "hhat_ready"))
        rh_ready, su_ready, keep_ready, take_ready, ah_ready, ah_hi_ready, ah_lo_ready = map(
            sem, ("rh_ready", "su_ready", "keep_ready", "take_ready", "ah_ready", "ah_hi_ready", "ah_lo_ready"))
        dnn1_done, dnn2_done, dnn3_done, dnn_step, var_ready, std_ready, y_ready, stored = map(
            sem, ("dnn1_done", "dnn2_done", "dnn3_done", "dnn_step", "var_ready", "std_ready", "y_ready", "stored"))

        def col(c, parts=P):
            return sm[0:parts, c:c + 1]

        def exists(i, k):
            return 0 <= RING * i + k < T if isinstance(i, int) else True

        def count(eng, semaphore, value):
            if not isinstance(value, int) or value > 0:
                eng.wait_ge(semaphore, value)

        def ends_group(i, k):
            return exists(i, k) and (k % G == G - 1 or (isinstance(i, int) and RING * i + k == T - 1))

        def group(i, k):
            return (RING // G) * i + k // G

        def run(eng, step):
            for k in range(FIRST):
                step(0, k)
            with eng.Fori(0, LOOPS) as i:
                for k in range(FIRST, FIRST + RING):
                    step(i, k)
            for k in range(FIRST, T + LAG - RING * LOOPS):
                step(LOOPS, k)

        block = ctx.enter_context(nc.Block())

        @block.sync
        def _(sp):
            sp.dma_start(idx_raw[:, 0:T, :], recent_idx).then_inc(idx_loaded, 16)
            sp.dma_start(fix_raw[:, 0, :], user_idx).then_inc(fix_idx_loaded, 16)
            sp.dma_start(fix_raw[:, 1, :], cand_idx).then_inc(fix_idx_loaded, 16)
            sp.dma_start(w[:, 0:INPUT, :], weights[:, 0:INPUT, :]).then_inc(input_w_loaded, 16)
            sp.dma_start(w[:, INPUT:SPLIT, :], weights[:, INPUT:SPLIT, :]).then_inc(w_loaded, 16)
            sp.dma_start(sm[:], small).then_inc(small_loaded, 16)
            sp.dma_start(w[:, SPLIT:WEIGHTS, :], weights[:, SPLIT:WEIGHTS, :]).then_inc(rest_w_loaded, 16)
            sp.dma_start(w1[:], att_w1).then_inc(att_loaded, 16)
            sp.dma_start(d2[:], dnn_w2).then_inc(dnn_loaded, 16)
            sp.dma_start(d3[:], dnn_w3).then_inc(dnn_loaded, 16)
            sp.wait_ge(diag_cleared, 2)
            for j in range(G):
                block_j = slice(A * j, A * (j + 1))
                sp.dma_start(w2_diag[block_j, block_j], att_w2).then_inc(att_loaded, 16)
                sp.dma_start(w3_diag[block_j, j:j + 1], att_w3).then_inc(att_loaded, 16)

            for g in range(-(-T // G)):
                sp.wait_ge(score_ready, g + 1)
                for j in range(G):
                    count(sp, spread[j], 16 * g)
                sp.dma_start(score_dram, score[:]).then_inc(score_stored, 16)
                sp.wait_ge(score_stored, 16 * g + 16)
                count(sp, su_ready, G * g - G)
                for j in range(min(G, T - G * g)):
                    sp.dma_start(score_all[:, g % 2, j, :], score_dram[j:j + 1, :].broadcast_to([P, B]))\
                        .then_inc(spread[j], 16)
            sp.wait_ge(y_ready, 1)
            sp.dma_start(out, y[:]).then_inc(stored, 16)
            sp.wait_ge(stored, 16)

        @block.gpsimd
        def _(pool):
            nc.gpsimd.iota(idx_off[:], pattern=[[CANDS, T + 2], [0, NC]], base=0,
                           channel_multiplier=0).then_inc(offsets_made, 1)
            nc.gpsimd.memset(identity[:], 0.0).then_inc(identity_step, 1)
            pool.wait_ge(identity_step, 1)
            nc.gpsimd.affine_select(out=identity[:], in_=identity[:], compare_op=ALU.not_equal, fill=1.0,
                                    base=0, pattern=[[-1, P]], channel_multiplier=1).then_inc(identity_step, 1)

            def place_indices(i, k):
                half = (k // AHEAD) % 2
                if not (isinstance(i, int) and RING * i + k < 2 * AHEAD):
                    last = k - AHEAD - 1
                    pool.wait_ge(gathered[last % RING], 16 * NC * (i + last // RING + 1))
                nc.gpsimd.tensor_copy(idx_now[:, half], idx_all[:, bass.ds(RING * i + k, AHEAD), :])\
                    .then_inc(idx_copied, 1)

            def gather(i, k, chunks=range(NC)):
                for c in chunks:
                    nc.gpsimd.indirect_dma_start(
                        rows[:, k % RING, c, :], None, recent_emb,
                        bass.IndirectOffsetOnAxis(ap=idx_now[:, (k // AHEAD) % 2, k % AHEAD, c:c + 1], axis=0))\
                        .then_inc(gathered[k % RING], 16)

            def gather_fixed(f, table):
                for c in range(NC):
                    nc.gpsimd.indirect_dma_start(
                        fix_rows[:, f, c, :], None, table,
                        bass.IndirectOffsetOnAxis(ap=fix_idx[:, f, c:c + 1], axis=0)).then_inc(fix_gathered[f], 16)

            pool.wait_ge(idx_ready, 1)
            place_indices(0, 0)
            place_indices(0, AHEAD)
            pool.wait_ge(idx_copied, 2)
            gather(0, 0)
            pool.wait_ge(idx_ready, 2)
            gather_fixed(1, cand_emb)
            for k in range(1, AHEAD):
                gather(0, k)

            def step(i, k):
                t = RING * i + k
                if (k + 1) % AHEAD == 0 and exists(i, k + 1 + AHEAD):
                    place_indices(i, k + 1 + AHEAD)
                    pool.wait_ge(idx_copied, (RING // AHEAD) * i + (k + 1) // AHEAD + 2)
                if exists(i, k):
                    pool.wait_ge(z_ready, t + 1)
                    count(pool, h_ready, t)
                    nc.gpsimd.tensor_tensor(zh[:], z[:], h[:, (k - 1) % RING, :], ALU.mult).then_inc(zh_ready, 1)
                if exists(i, k + AHEAD):
                    gather(i, k + AHEAD, (0, 1))
                if exists(i, k - LAG):
                    s = t - LAG
                    pool.wait_ge(spread[(k - LAG) % G], 16 * group(i, k - LAG) + 16)
                    pool.wait_ge(au_ready, s + 1)
                    nc.gpsimd.tensor_tensor(su[:], au[:], score_all[:, ((k - LAG) // G) % 2, (k - LAG) % G, :],
                                            ALU.mult).then_inc(su_ready, 1)
                if exists(i, k):
                    pool.wait_ge(h_ready, t + 1)
                    if k % G == 0:
                        count(pool, att1_done, group(i, k))
                    nc.gpsimd.tensor_tensor(hc[:, k % G, :], h[:, k % RING, :], cand_t[:], ALU.mult)\
                        .then_inc(hc_ready, 1)
                if exists(i, k + AHEAD):
                    gather(i, k + AHEAD, (2, 3))
                if isinstance(i, int) and t == T - AHEAD:
                    gather_fixed(0, user_emb)

            pool.wait_ge(fix_copied, 1)
            pool.wait_ge(states_zeroed, 6)
            run(pool, step)

        @block.scalar
        def _(act):
            def split_x(i, k):
                act.wait_ge(x_turned, RING * i + k + 1)
                nc.scalar.activation(x_hi[:, k % 2, :], ps_x[:], ACT.Copy).then_inc(x_hi_ready, 1)

            split_x(0, 0)
            act.wait_ge(small_loaded, 16)
            act.wait_ge(bias_ready, 4)
            act.wait_ge(fix_turned, 1)
            nc.scalar.activation(cand_t[:], ps_att[:], ACT.Copy).then_inc(fix_copied, 1)
            split_x(0, 1)

            def step(i, k):
                t = RING * i + k
                s = t - LAG
                gru, aug = exists(i, k), exists(i, k - LAG)
                if ends_group(i, k - 2):
                    g = group(i, k - 2)
                    act.wait_ge(att3_done, g + 1)
                    count(act, score_stored, 16 * g)
                    nc.scalar.activation(score[:], ps_att[0:G, :], ACT.Sigmoid, bias=col(ATT_B3, G))\
                        .then_inc(score_ready, 1)
                if gru:
                    act.wait_ge(r_done, t + 1)
                    nc.scalar.activation(r[:], ps_r[:], ACT.Sigmoid, bias=bias_r[:]).then_inc(r_ready, 1)
                    act.wait_ge(z_done, t + 1)
                    nc.scalar.activation(z[:], ps_z[:], ACT.Sigmoid, bias=bias_z[:]).then_inc(z_ready, 1)
                if aug:
                    act.wait_ge(ar_done, s + 1)
                    nc.scalar.activation(ar[:], ps_a[:], ACT.Sigmoid, bias=col(AUG_R)).then_inc(ar_ready, 1)
                if gru:
                    act.wait_ge(n_pre_ready, t + 1)
                    nc.scalar.activation(n[:], n_pre[:], ACT.Tanh, bias=col(IH_N)).then_inc(n_ready, 1)
                if exists(i, k + 2):
                    split_x(i, k + 2)
                if aug:
                    act.wait_ge(au_done, s + 1)
                    nc.scalar.activation(au[:], ps_au[:], ACT.Sigmoid, bias=col(AUG_U)).then_inc(au_ready, 1)
                if gru:
                    act.wait_ge(h_ready, t + 1)
                    nc.scalar.activation(h_hi[:, k % RING, :], h[:, k % RING, :], ACT.Copy).then_inc(h_hi_ready, 1)
                if ends_group(i, k - 1):
                    act.wait_ge(att2_done, group(i, k - 1) + 1)
                    nc.scalar.activation(att_p2[:], ps_att[:], ACT.Relu, bias=col(ATT_B2)).then_inc(p2_ready, 1)
                    nc.scalar.activation(att_n2[:], ps_att[:], ACT.Relu, bias=att_nb2[:], scale=-1.0).then_inc(n2_ready, 1)
                if aug:
                    act.wait_ge(ah_done, s + 1)
                    nc.scalar.activation(hhat[:], ps_a[:], ACT.Tanh, bias=col(AUG_H)).then_inc(hhat_ready, 1)

            run(act, step)
            act.wait_ge(fix_turned, 2)
            nc.scalar.activation(user_t[:], ps_x[:], ACT.Copy).then_inc(fix_copied, 1)
            for layer, parts in ((0, P), (1, H2)):
                act.wait_ge(var_ready, layer + 1)
                nc.scalar.activation(std[0:parts], var_eps[0:parts], ACT.Sqrt).then_inc(std_ready, 1)

        @block.vector
        def _(dve):
            nc.vector.memset(idx_all[:], 0).then_inc(idx_step, 1)
            steps = 1

            def idx_op(ins):
                nonlocal steps
                steps += 1
                ins.then_inc(idx_step, 1)
                dve.wait_ge(idx_step, steps)

            dve.wait_ge(idx_loaded, 16)
            idx_op(nc.vector.tensor_scalar(idx_neg[:, 0:T, :], idx_raw[:, 0:T, :], 0.0, float(CANDS), ALU.is_lt, ALU.mult))
            idx_op(nc.vector.tensor_tensor(idx_flt[:, 0:T, :], idx_raw[:, 0:T, :], idx_neg[:, 0:T, :], ALU.add))
            idx_op(nc.vector.tensor_scalar(idx_flt[:, 0:T, :], idx_flt[:, 0:T, :], 0.0, float(CANDS - 1), ALU.max, ALU.min))
            dve.wait_ge(offsets_made, 1)
            nc.vector.tensor_tensor(idx_all[:, 0:T, :], idx_flt[:, 0:T, :], idx_off[:, 0:T, :], ALU.add)\
                .then_inc(idx_ready, 1)
            dve.wait_ge(fix_idx_loaded, 32)
            for f, size in enumerate((USERS, CANDS)):
                idx_op(nc.vector.tensor_scalar(fix_neg[:, f, :], fix_raw[:, f, :], 0.0, float(size), ALU.is_lt, ALU.mult))
                idx_op(nc.vector.tensor_tensor(fix_flt[:, f, :], fix_raw[:, f, :], fix_neg[:, f, :], ALU.add))
                last = nc.vector.tensor_scalar(fix_idx[:, f, :], fix_flt[:, f, :], 0.0, float(size - 1), ALU.max, ALU.min)
            last.then_inc(idx_ready, 1)

            nc.vector.memset(w2_diag[:], 0.0).then_inc(diag_cleared, 1)
            nc.vector.memset(w3_diag[:], 0.0).then_inc(diag_cleared, 1)
            parts = (slice(0, INPUT), slice(INPUT, SPLIT))
            for part, arrived in zip(parts, (input_w_loaded, w_loaded)):
                dve.wait_ge(arrived, 16)
                nc.vector.tensor_copy(w_hi[:, part, :], w[:, part, :]).then_inc(setup_step, 1)
                dve.wait_ge(setup_step, 1 if part is parts[0] else 2)
                nc.vector.tensor_tensor(w_lo[:, part, :], w[:, part, :], w_hi[:, part, :].bitcast(fp32),
                                        ALU.subtract).then_inc(w_ready, 1)
            nc.vector.memset(h[:, RING - 1, :], 0.0).then_inc(states_zeroed, 1)
            nc.vector.memset(ah[:, 1, :], 0.0).then_inc(states_zeroed, 1)
            for state in (h_hi[:, RING - 1, :], h_lo[:, RING - 1, :], ah_hi[:], ah_lo[:]):
                nc.vector.memset(state.bitcast(fp32), 0.0).then_inc(states_zeroed, 1)

            def split_x(i, k):
                dve.wait_ge(x_hi_ready, RING * i + k + 1)
                nc.vector.tensor_tensor(x_lo[:, k % 2, :], ps_x[:], x_hi[:, k % 2, :].bitcast(fp32),
                                        ALU.subtract).then_inc(x_lo_ready, 1)

            dve.wait_ge(small_loaded, 16)
            nc.vector.tensor_tensor(bias_r[:], col(IH_R), col(HH_R), ALU.add).then_inc(bias_ready, 1)
            nc.vector.tensor_tensor(bias_z[:], col(IH_Z), col(HH_Z), ALU.add).then_inc(bias_ready, 1)
            nc.vector.tensor_scalar(att_nb2[:], col(ATT_B2), -1.0, None, ALU.mult).then_inc(bias_ready, 1)
            nc.vector.tensor_scalar(att_na2[:], col(ATT_A2), -1.0, None, ALU.mult).then_inc(bias_ready, 1)
            dve.wait_ge(att_loaded, 16 * (1 + 2 * G))
            nc.vector.tensor_tensor(w1_hs[:], w1[:, 0, :], w1[:, 2, :], ALU.add)
            for j in range(G):
                last = nc.vector.tensor_tensor(w1_c[:, j, :], w1[:, 1, :], w1[:, 2, :], ALU.subtract)
            last.then_inc(att_w_ready, 1)
            split_x(0, 0)
            dve.wait_ge(cand_done, 1)
            nc.vector.tensor_scalar(att_c[:], ps_au[:], col(ATT_B1), None, ALU.add).then_inc(att_c_ready, 1)

            split_x(0, 1)

            def step(i, k):
                t = RING * i + k
                s = t - LAG
                gru, aug = exists(i, k), exists(i, k - LAG)
                slot = k % RING
                if gru:
                    dve.wait_ge(nh_done, t + 1)
                    dve.wait_ge(r_ready, t + 1)
                    nc.vector.scalar_tensor_tensor(out=rhn[:], in0=ps_nh[:], scalar=col(HH_N), in1=r[:],
                                                   op0=ALU.add, op1=ALU.mult).then_inc(rhn_ready, 1)
                    dve.wait_ge(nx_done, t + 1)
                    dve.wait_ge(rhn_ready, t + 1)
                    nc.vector.tensor_tensor(n_pre[:], ps_nx[:], rhn[:], ALU.add).then_inc(n_pre_ready, 1)
                if ends_group(i, k - 1):
                    g = group(i, k - 1)
                    dve.wait_ge(att1_done, g + 1)
                    nc.vector.tensor_tensor(att_v1[:], ps_att[:], att_c[:], ALU.add).then_inc(v1_ready, 1)
                    dve.wait_ge(v1_ready, g + 1)
                    nc.vector.tensor_scalar(att_n1[:], att_v1[:], 0.0, col(ATT_A1), ALU.min, ALU.mult).then_inc(n1_ready, 1)
                if aug:
                    old = ah[:, (k - LAG - 1) % 2, :]
                    dve.wait_ge(ar_ready, s + 1)
                    count(dve, ah_ready, s)
                    nc.vector.tensor_tensor(rh[:], ar[:], old, ALU.mult).then_inc(rh_ready, 1)
                if gru:
                    dve.wait_ge(n_ready, t + 1)
                    nc.vector.scalar_tensor_tensor(out=zn[:], in0=z[:], scalar=1.0, in1=n[:],
                                                   op0=ALU.subtract, op1=ALU.mult).then_inc(zn_ready, 1)
                if ends_group(i, k - 1):
                    dve.wait_ge(n1_ready, g + 1)
                    nc.vector.scalar_tensor_tensor(out=att_o1[:], in0=att_v1[:], scalar=0.0, in1=att_n1[:],
                                                   op0=ALU.max, op1=ALU.add).then_inc(o1_ready, 1)
                if gru:
                    dve.wait_ge(zh_ready, t + 1)
                    dve.wait_ge(zn_ready, t + 1)
                    nc.vector.tensor_tensor(h[:, slot, :], zh[:], zn[:], ALU.subtract).then_inc(h_ready, 1)
                if exists(i, k + 2):
                    split_x(i, k + 2)
                if gru:
                    dve.wait_ge(h_ready, t + 1)
                    dve.wait_ge(h_hi_ready, t + 1)
                    nc.vector.tensor_tensor(h_lo[:, slot, :], h[:, slot, :], h_hi[:, slot, :].bitcast(fp32),
                                            ALU.subtract).then_inc(h_lo_ready, 1)
                if ends_group(i, k - 1):
                    dve.wait_ge(p2_ready, g + 1)
                    dve.wait_ge(n2_ready, g + 1)
                    nc.vector.scalar_tensor_tensor(out=att_o2[:], in0=att_n2[:], scalar=att_na2[:], in1=att_p2[:],
                                                   op0=ALU.mult, op1=ALU.add).then_inc(o2_ready, 1)
                if aug:
                    new = ah[:, (k - LAG) % 2, :]
                    dve.wait_ge(su_ready, s + 1)
                    nc.vector.scalar_tensor_tensor(out=keep[:], in0=su[:], scalar=1.0, in1=old,
                                                   op0=ALU.subtract, op1=ALU.mult).then_inc(keep_ready, 1)
                    dve.wait_ge(hhat_ready, s + 1)
                    nc.vector.tensor_tensor(take[:], su[:], hhat[:], ALU.mult).then_inc(take_ready, 1)
                    dve.wait_ge(keep_ready, s + 1)
                    dve.wait_ge(take_ready, s + 1)
                    nc.vector.tensor_tensor(new, take[:], keep[:], ALU.subtract).then_inc(ah_ready, 1)
                    dve.wait_ge(ah_ready, s + 1)
                    nc.vector.tensor_copy(ah_hi[:], new).then_inc(ah_hi_ready, 1)
                    dve.wait_ge(ah_hi_ready, s + 1)
                    nc.vector.tensor_tensor(ah_lo[:], new, ah_hi[:].bitcast(fp32), ALU.subtract).then_inc(ah_lo_ready, 1)

            run(dve, step)

            done = 0

            def link(ins):
                nonlocal done
                done += 1
                ins.then_inc(dnn_step, 1)
                dve.wait_ge(dnn_step, done)

            for layer, (parts, ps, made, b, g_, b_, a, dst) in enumerate((
                    (P, ps_r, dnn1_done, DNN_B1, BN1_G, BN1_B, DNN_A1, dz1),
                    (H2, ps_z, dnn2_done, DNN_B2, BN2_G, BN2_B, DNN_A2, dz2))):
                on = slice(0, parts)
                dve.wait_ge(made, 1)
                link(nc.vector.tensor_scalar(dx[on], ps[on], col(b, parts), None, ALU.add))
                link(nc.vector.bn_stats(stats[on], dx[on]))
                link(nc.vector.bn_aggr(aggr[on], stats[on]))
                nc.vector.tensor_scalar(var_eps[on], aggr[on, 1:2], EPS, None, ALU.add).then_inc(var_ready, 1)
                dve.wait_ge(std_ready, layer + 1)
                link(nc.vector.reciprocal(rstd[on], std[on]))
                link(nc.vector.tensor_tensor(gain[on], rstd[on], col(g_, parts), ALU.mult))
                link(nc.vector.tensor_tensor(mgain[on], aggr[on, 0:1], gain[on], ALU.mult))
                link(nc.vector.tensor_tensor(shift[on], col(b_, parts), mgain[on], ALU.subtract))
                link(nc.vector.tensor_scalar(dy[on], dx[on], gain[on], shift[on], ALU.mult, ALU.add))
                link(nc.vector.tensor_scalar(dn[on], dy[on], 0.0, col(a, parts), ALU.min, ALU.mult))
                link(nc.vector.scalar_tensor_tensor(out=dst[on], in0=dy[on], scalar=0.0, in1=dn[on],
                                                    op0=ALU.max, op1=ALU.add))
            dve.wait_ge(dnn3_done, 1)
            nc.vector.tensor_scalar(y[:], ps_nx[0:1, :], col(DNN_B3, 1), None, ALU.add).then_inc(y_ready, 1)

        @block.tensor
        def _(pe):
            mm = nc.tensor.matmul

            def turn(src, ps, semaphore):
                for c in range(NC):
                    last = nc.tensor.transpose(ps[:, c * P:(c + 1) * P], src[:, c, :], identity[:])
                last.then_inc(semaphore, 1)

            def turn_x(i, k):
                pe.wait_ge(gathered[k % RING], 16 * NC * (i + k // RING + 1))
                turn(rows[:, k % RING], ps_x, x_turned)

            def exact(ps, block_, hi, lo, start, stop):
                mm(ps[:], w_hi[:, block_, :], hi, start=start, stop=False)
                mm(ps[:], w_lo[:, block_, :], hi, start=False, stop=False)
                return mm(ps[:], w_hi[:, block_, :], lo, start=False, stop=stop)

            def input_gate(i, k, ps, block_, read, closed):
                pe.wait_ge(x_lo_ready, RING * i + k + 1)
                count(pe, read, RING * i + k)
                return exact(ps, block_, x_hi[:, k % 2, :], x_lo[:, k % 2, :], True, closed)

            pe.wait_ge(identity_step, 2)
            turn_x(0, 0)
            pe.wait_ge(w_ready, 2)
            input_gate(0, 0, ps_r, W_IR, r_ready, False)
            input_gate(0, 0, ps_nx, W_IN, n_pre_ready, True).then_inc(nx_done, 1)
            input_gate(0, 0, ps_z, W_IZ, z_ready, False)
            pe.wait_ge(fix_gathered[1], 16 * NC)
            turn(fix_rows[:, 1], ps_att, fix_turned)
            pe.wait_ge(fix_copied, 1)
            pe.wait_ge(att_w_ready, 1)
            mm(ps_au[:], w1_c[:].rearrange("p g a -> p (g a)"), cand_t[:], start=True, stop=True).then_inc(cand_done, 1)
            turn_x(0, 1)
            pe.wait_ge(states_zeroed, 6)
            pe.wait_ge(rest_w_loaded, 16)

            def step(i, k):
                t = RING * i + k
                s = t - LAG
                gru, aug = exists(i, k), exists(i, k - LAG)
                prev = (k - 1) % RING
                if aug:
                    slot = (k - LAG) % RING
                    state_hi, state_lo = h_hi[:, slot, :], h_lo[:, slot, :]
                    count(pe, au_ready, s)
                    exact(ps_au, W_AUX, state_hi, state_lo, True, False)
                if gru:
                    hi, lo = h_hi[:, prev, :], h_lo[:, prev, :]
                    count(pe, h_hi_ready, t)
                    count(pe, rhn_ready, t)
                    mm(ps_nh[:], w_hi[:, W_HN, :], hi, start=True, stop=False)
                    mm(ps_nh[:], w_lo[:, W_HN, :], hi, start=False, stop=False)
                    mm(ps_r[:], w_hi[:, W_HR, :], hi, start=False, stop=False)
                    mm(ps_r[:], w_lo[:, W_HR, :], hi, start=False, stop=False)
                    count(pe, h_lo_ready, t)
                    mm(ps_r[:], w_hi[:, W_HR, :], lo, start=False, stop=True).then_inc(r_done, 1)
                    mm(ps_nh[:], w_hi[:, W_HN, :], lo, start=False, stop=True).then_inc(nh_done, 1)
                    exact(ps_z, W_HZ, hi, lo, False, True).then_inc(z_done, 1)
                if ends_group(i, k - 2):
                    pe.wait_ge(o2_ready, group(i, k - 2) + 1)
                    mm(ps_att[0:G, :], w3_diag[:], att_o2[:], start=True, stop=True).then_inc(att3_done, 1)
                if aug:
                    count(pe, hhat_ready, s)
                    exact(ps_a, W_ARX, state_hi, state_lo, True, False)
                if ends_group(i, k - 1):
                    g = group(i, k - 1)
                    first = k - 1 - (k - 1) % G
                    count(pe, score_ready, g)
                    pe.wait_ge(hc_ready, t)
                    for j in range(G):
                        mm(ps_att[A * j:A * (j + 1), :], w1_hs[:], h[:, (first + j) % RING, :], start=True, stop=False)
                    for j in range(G):
                        last = mm(ps_att[A * j:A * (j + 1), :], w1[:, 3, :], hc[:, j, :], start=False, stop=True)
                    last.then_inc(att1_done, 1)
                if exists(i, k + 2):
                    count(pe, x_lo_ready, t + 2)
                    turn_x(i, k + 2)
                if aug:
                    count(pe, ah_hi_ready, s)
                    mm(ps_a[:], w_hi[:, W_ARH, :], ah_hi[:], start=False, stop=False)
                    mm(ps_a[:], w_lo[:, W_ARH, :], ah_hi[:], start=False, stop=False)
                    count(pe, ah_lo_ready, s)
                    mm(ps_a[:], w_hi[:, W_ARH, :], ah_lo[:], start=False, stop=True).then_inc(ar_done, 1)
                    exact(ps_au, W_AUH, ah_hi[:], ah_lo[:], False, True).then_inc(au_done, 1)
                if exists(i, k + 1):
                    input_gate(i, k + 1, ps_r, W_IR, r_ready, False)
                    input_gate(i, k + 1, ps_nx, W_IN, n_pre_ready, True).then_inc(nx_done, 1)
                if aug:
                    pe.wait_ge(ar_ready, s + 1)
                    exact(ps_a, W_AHX, state_hi, state_lo, True, False)
                    pe.wait_ge(rh_ready, s + 1)
                    mm(ps_a[:], w[:, W_AHH, :], rh[:], start=False, stop=True).then_inc(ah_done, 1)
                if ends_group(i, k - 1):
                    pe.wait_ge(o1_ready, g + 1)
                    mm(ps_att[:], w2_diag[:], att_o1[:], start=True, stop=True).then_inc(att2_done, 1)
                if exists(i, k + 1):
                    input_gate(i, k + 1, ps_z, W_IZ, z_ready, False)

            run(pe, step)
            pe.wait_ge(fix_gathered[0], 16 * NC)
            turn(fix_rows[:, 0], ps_x, fix_turned)
            pe.wait_ge(fix_copied, 2)
            mm(ps_r[:], w[:, W_DU, :], user_t[:], start=True, stop=False)
            mm(ps_r[:], w[:, W_DC, :], cand_t[:], start=False, stop=False)
            pe.wait_ge(ah_ready, T)
            mm(ps_r[:], w[:, W_DH, :], ah[:, (T - 1) % 2, :], start=False, stop=True).then_inc(dnn1_done, 1)
            pe.wait_ge(dnn_loaded, 32)
            pe.wait_ge(dnn_step, 10)
            mm(ps_z[0:H2, :], d2[:], dz1[:], start=True, stop=True).then_inc(dnn2_done, 1)
            pe.wait_ge(dnn_step, 20)
            mm(ps_nx[0:1, :], d3[:], dz2[:], start=True, stop=True).then_inc(dnn3_done, 1)


def kernel(**inputs):
    import numpy as np
    import concourse.bacc as bacc
    from concourse.bass_utils import run_bass_kernel_spmd

    x = {name.replace("L0_rec_", ""): np.asarray(a) for name, a in inputs.items()}

    def rows_of(a, n):
        return a.reshape(n, P, a.shape[1]).transpose(1, 0, 2)

    def chunks(idx):
        return np.ascontiguousarray(idx.reshape(NC, P, -1).transpose(1, 2, 0))

    ih, hh = rows_of(x["gru_W_ih"], 3), rows_of(x["gru_W_hh"], 3)
    wr, wu, wh = (rows_of(x[k], 2) for k in ("aug_Wr", "aug_Wu", "aug_Wh"))
    dnn = rows_of(x["dnn_W1"], 3)
    weights = np.empty((P, WEIGHTS, P), np.float32)
    for block, a in ((W_IR, ih[:, 0].T), (W_IZ, ih[:, 1].T), (W_IN, ih[:, 2].T),
                     (W_HR, hh[:, 0].T), (W_HZ, hh[:, 1].T), (W_HN, hh[:, 2].T),
                     (W_ARX, wr[:, 0]), (W_ARH, wr[:, 1]), (W_AUX, wu[:, 0]), (W_AUH, wu[:, 1]),
                     (W_AHH, wh[:, 0]), (W_AHX, wh[:, 1]), (W_DU, dnn[:, 0]), (W_DC, dnn[:, 1]), (W_DH, dnn[:, 2])):
        weights[:, block] = a
    small = np.zeros((P, SMALL), np.float32)
    for c, a in ((IH_R, x["gru_b_ih"][0:P]), (IH_Z, x["gru_b_ih"][P:2 * P]), (IH_N, x["gru_b_ih"][2 * P:]),
                 (HH_R, x["gru_b_hh"][0:P]), (HH_Z, x["gru_b_hh"][P:2 * P]), (HH_N, x["gru_b_hh"][2 * P:]),
                 (AUG_R, x["aug_br"]), (AUG_U, x["aug_bu"]), (AUG_H, x["aug_bh"]),
                 (DNN_B1, x["dnn_b1"]), (BN1_G, x["bn1_g"]), (BN1_B, x["bn1_b"]),
                 (ATT_B1, np.tile(x["att_b1"], G)), (ATT_B2, np.tile(x["att_b2"], G)),
                 (DNN_B2, x["dnn_b2"]), (BN2_G, x["bn2_g"]), (BN2_B, x["bn2_b"])):
        small[0:a.shape[0], c] = a
    for c, name in ((ATT_A1, "att_a1"), (ATT_A2, "att_a2"), (DNN_A1, "dnn_a1"), (DNN_A2, "dnn_a2"),
                    (ATT_B3, "att_b3"), (DNN_B3, "dnn_b3")):
        small[:, c] = x[name].reshape(())
    arrays = {
        "recent_idx": chunks(x["r_recent_features"]),
        "user_idx": chunks(x["r_user_features"])[:, 0],
        "cand_idx": chunks(x["r_candidate_features"])[:, 0],
        "user_emb": x["user_emb"],
        "cand_emb": x["cand_emb"],
        "recent_emb": x["recent_emb"].reshape(T * CANDS, P),
        "weights": weights,
        "small": small,
        "att_w1": rows_of(x["att_W1"], 4),
        "att_w2": x["att_W2"],
        "att_w3": x["att_W3"],
        "dnn_w2": x["dnn_W2"],
        "dnn_w3": x["dnn_W3"],
    }
    arrays = {name: np.ascontiguousarray(a) for name, a in arrays.items()}

    nc = bacc.Bacc("TRN2", target_bir_lowering=False, num_devices=1)
    aps = {name: nc.dram_tensor(name, a.shape, mybir.dt.from_np(a.dtype), kind="ExternalInput").ap()
           for name, a in arrays.items()}
    out = nc.dram_tensor("out", (1, B), mybir.dt.float32, kind="ExternalOutput").ap()
    recommender(nc, **aps, out=out)
    result = run_bass_kernel_spmd(nc, [arrays], core_ids=[0])
    return result.results[0]["out"].reshape(B, 1)
```

```python
import concourse.bass as bass
from concourse import mybir
from contextlib import ExitStack


B = 512
P = 128
NC = B // P
T = 50
CANDS = 2500
USERS = 12500
H2 = 64
A = 32
G = P // A
LAG = 5
FIRST = LAG + 1
RING = 8
AHEAD = 4
LOOPS = (T - FIRST - AHEAD) // RING
WHOLE = T - LAG
HALVES = (slice(0, B // 2), slice(B // 2, B))
EPS = 1e-5

(IH_R, IH_Z, IH_N, HH_R, HH_Z, HH_N, AUG_R, AUG_U, AUG_H, BN1_G, BN1_B, ATT_B1, ATT_B2,
 BN2_G, BN2_B, ATT_A1, ATT_A2, DNN_A1, DNN_A2, ATT_B3, DNN_B3, SMALL) = range(22)
(W_IR, W_IZ, W_IN, W_HR, W_HZ, W_HN, W_ARX, W_AUX, W_AHX, W_ARH, W_AUH, W_AHH,
 W_DU, W_DC, W_DH, WEIGHTS) = range(16)
SPLIT = W_AHH + 1
INPUT = W_IN + 1


def recommender(nc, recent_idx, user_idx, cand_idx, user_emb, cand_emb, recent_emb,
                weights, small, att_w1, att_w2, att_w3, dnn_w2, dnn_w3, dnn_bias, out):
    fp32 = mybir.dt.float32
    fp32r = mybir.dt.float32r
    i32 = mybir.dt.int32
    ALU = mybir.AluOpType
    ACT = mybir.ActivationFunctionType

    with ExitStack() as ctx:
        def sb(name, shape, dt=fp32):
            return ctx.enter_context(nc.sbuf_tensor(name, shape, dt))

        def sem(name):
            return ctx.enter_context(nc.semaphore(name))

        w = sb("w", [P, WEIGHTS, P])
        w_hi = sb("w_hi", [P, SPLIT, P], fp32r)
        w_lo = sb("w_lo", [P, SPLIT, P], fp32r)
        sm = sb("sm", [P, SMALL])
        bias_r = sb("bias_r", [P, 1])
        bias_z = sb("bias_z", [P, 1])
        att_nb2 = sb("att_nb2", [P, 1])
        att_na2 = sb("att_na2", [P, 1])
        w1 = sb("w1", [P, 4, A])
        w1_hs = sb("w1_hs", [P, A])
        w1_c = sb("w1_c", [P, G, A])
        w2_diag = sb("w2_diag", [P, P])
        w3_diag = sb("w3_diag", [P, G])
        d2 = sb("d2", [P, H2])
        d3 = sb("d3", [H2, 1])
        identity = sb("identity", [P, P])

        idx_raw = sb("idx_raw", [P, T + 2, NC], i32)
        idx_off = sb("idx_off", [P, T + 2, NC], i32)
        idx_neg = sb("idx_neg", [P, T + 2, NC])
        idx_flt = sb("idx_flt", [P, T + 2, NC])
        idx_all = sb("idx_all", [P, T + 2, NC], i32)
        idx_now = sb("idx_now", [P, 2, AHEAD, NC], i32)
        fix_raw = sb("fix_raw", [P, 2, NC], i32)
        fix_neg = sb("fix_neg", [P, 2, NC])
        fix_flt = sb("fix_flt", [P, 2, NC])
        fix_idx = sb("fix_idx", [P, 2, NC], i32)

        rows = sb("rows", [P, RING, NC, P])
        fix_rows = sb("fix_rows", [P, 2, NC, P])
        x_hi = sb("x_hi", [P, 2, B], fp32r)
        x_lo = sb("x_lo", [P, 2, B], fp32r)
        user_t = sb("user_t", [P, B])
        cand_t = sb("cand_t", [P, B])

        h = sb("h", [P, RING, B])
        h_hi = sb("h_hi", [P, RING, B], fp32r)
        h_lo = sb("h_lo", [P, RING, B], fp32r)
        r = sb("r", [P, B])
        z = sb("z", [P, B])
        rhn = sb("rhn", [P, B])
        n_pre = sb("n_pre", [P, B])
        n = sb("n", [P, B])
        zh = sb("zh", [P, B])
        zn = sb("zn", [P, B])
        hc = sb("hc", [P, G, B])

        att_c = sb("att_c", [P, B])
        att_v1 = sb("att_v1", [P, B])
        att_n1 = sb("att_n1", [P, B])
        att_o1 = sb("att_o1", [P, B])
        att_p2 = sb("att_p2", [P, B])
        att_n2 = sb("att_n2", [P, B])
        att_o2 = sb("att_o2", [P, B])
        score = sb("score", [G, B])
        score_all = sb("score_all", [P, 2, G, B])
        score_dram = nc.dram_tensor("score_dram", [G, B], fp32, kind="Internal").ap()

        ah = sb("ah", [P, 2, B])
        ah_hi = sb("ah_hi", [P, B], fp32r)
        ah_lo = sb("ah_lo", [P, B], fp32r)
        ar = sb("ar", [P, B])
        au = sb("au", [P, B])
        su = sb("su", [P, B])
        su0 = sb("su0", [P, B // 2])
        rh = sb("rh", [P, B])
        rh_hi = sb("rh_hi", [P, B], fp32r)
        rh_lo = sb("rh_lo", [P, B], fp32r)
        hhat = sb("hhat", [P, B])
        keep = sb("keep", [P, B])
        take = sb("take", [P, B])

        dy = sb("dy", [P, B])
        dn = sb("dn", [P, B])
        dz1 = sb("dz1", [P, B])
        dz2 = sb("dz2", [H2, B])
        stats = sb("stats", [P, 6])
        aggr = sb("aggr", [P, 2])
        eps = sb("eps", [P, 1])
        table_touch = sb("table_touch", [P, 1])
        std = sb("std", [P, 1])
        rstd = sb("rstd", [P, 1])
        gain = sb("gain", [P, 1])
        offset = sb("offset", [P, 1])
        ones = sb("ones", [1, B])
        bias_rows = sb("bias_rows", [1, P + H2])
        y = sb("y", [1, B])

        def bank(name):
            return ctx.enter_context(nc.psum_tensor(name, [P, B], fp32))

        ps_r, ps_z, ps_nx, ps_nh = bank("ps_r"), bank("ps_z"), bank("ps_nx"), bank("ps_nh")
        ps_x, ps_att, ps_au = bank("ps_x"), bank("ps_att"), bank("ps_au")
        ps_a = bank("ps_a")

        fix_idx_loaded, input_w_loaded, rest_w_loaded = map(
            sem, ("fix_idx_loaded", "input_w_loaded", "rest_w_loaded"))
        idx_loaded, small_loaded, w_loaded, att_loaded, dnn_loaded = map(
            sem, ("idx_loaded", "small_loaded", "w_loaded", "att_loaded", "dnn_loaded"))
        diag_cleared, identity_step, offsets_made = map(sem, ("diag_cleared", "identity_step", "offsets_made"))
        idx_step, idx_ready, idx_copied = map(sem, ("idx_step", "idx_ready", "idx_copied"))
        gathered = [sem(f"gathered{s}") for s in range(RING)]
        fix_gathered = [sem("user_gathered"), sem("cand_gathered")]
        aug_zeroed, table_loaded = map(sem, ("aug_zeroed", "table_loaded"))
        setup_step, w_ready, bias_ready, gru_zeroed = map(
            sem, ("setup_step", "w_ready", "bias_ready", "gru_zeroed"))
        fix_turned, fix_copied, cand_done, att_c_ready, att_w_ready = map(
            sem, ("fix_turned", "fix_copied", "cand_done", "att_c_ready", "att_w_ready"))
        x_turned, x_hi_ready, x_lo_ready = map(sem, ("x_turned", "x_hi_ready", "x_lo_ready"))
        nx_done, r_done, nh_done, z_done = map(sem, ("nx_done", "r_done", "nh_done", "z_done"))
        r_ready, z_ready, n_ready = map(sem, ("r_ready", "z_ready", "n_ready"))
        rhn_ready, n_pre_ready, zh_ready, zn_ready = map(sem, ("rhn_ready", "n_pre_ready", "zh_ready", "zn_ready"))
        h_ready, h_hi_ready, h_lo_ready, hc_ready = map(sem, ("h_ready", "h_hi_ready", "h_lo_ready", "hc_ready"))
        att1_done, att2_done, att3_done = map(sem, ("att1_done", "att2_done", "att3_done"))
        v1_ready, n1_ready, o1_ready, p2_ready, n2_ready, o2_ready = map(
            sem, ("v1_ready", "n1_ready", "o1_ready", "p2_ready", "n2_ready", "o2_ready"))
        score_ready, score_stored = map(sem, ("score_ready", "score_stored"))
        spread = [sem(f"spread{j}") for j in range(G)]
        ar_done, au_done, ah_done = map(sem, ("ar_done", "au_done", "ah_done"))
        ar_ready, au_ready, hhat_ready = map(sem, ("ar_ready", "au_ready", "hhat_ready"))
        rh_ready, su_ready, keep_ready, take_ready, ah_ready, ah_hi_ready, ah_lo_ready = map(
            sem, ("rh_ready", "su_ready", "keep_ready", "take_ready", "ah_ready", "ah_hi_ready", "ah_lo_ready"))
        rh_hi_ready, rh_lo_ready, su0_ready, constants_set, dnn_made = map(
            sem, ("rh_hi_ready", "rh_lo_ready", "su0_ready", "constants_set", "dnn_made"))
        dnn1_done, dnn2_done, dnn3_done, dnn_step, var_ready, std_ready, y_ready, stored = map(
            sem, ("dnn1_done", "dnn2_done", "dnn3_done", "dnn_step", "var_ready", "std_ready", "y_ready", "stored"))

        def col(c, parts=P):
            return sm[0:parts, c:c + 1]

        def exists(i, k):
            return 0 <= RING * i + k < T if isinstance(i, int) else True

        def count(eng, semaphore, value):
            if not isinstance(value, int) or value > 0:
                eng.wait_ge(semaphore, value)

        def ends_group(i, k):
            return exists(i, k) and (k % G == G - 1 or (isinstance(i, int) and RING * i + k == T - 1))

        def group(i, k):
            return (RING // G) * i + k // G

        def opening(i, k):
            return isinstance(i, int) and RING * i + k < LAG

        def pieces(gru):
            if gru:
                return ((slice(0, B), ps_a, ps_a),)
            return (HALVES[0], ps_a, ps_nh), (HALVES[1], ps_z, ps_nx)

        def aug_count(s, piece=1):
            if isinstance(s, int) and s >= WHOLE:
                return WHOLE + 2 * (s - WHOLE) + piece + 1
            return s + 1

        def run(eng, step):
            for k in range(FIRST):
                step(0, k)
            with eng.Fori(0, LOOPS) as i:
                for k in range(FIRST, FIRST + RING):
                    step(i, k)
            for k in range(FIRST, T + LAG - RING * LOOPS):
                step(LOOPS, k)

        block = ctx.enter_context(nc.Block())

        @block.sync
        def _(sp):
            sp.dma_start(idx_raw[:, 0:T, :], recent_idx).then_inc(idx_loaded, 16)
            sp.dma_start(fix_raw[:, 0, :], user_idx).then_inc(fix_idx_loaded, 16)
            sp.dma_start(fix_raw[:, 1, :], cand_idx).then_inc(fix_idx_loaded, 16)
            sp.dma_start(w[:, 0:INPUT, :], weights[:, 0:INPUT, :]).then_inc(input_w_loaded, 16)
            sp.dma_start(w[:, INPUT:SPLIT, :], weights[:, INPUT:SPLIT, :]).then_inc(w_loaded, 16)
            sp.dma_start(sm[:], small).then_inc(small_loaded, 16)
            sp.dma_start(w[:, SPLIT:WEIGHTS, :], weights[:, SPLIT:WEIGHTS, :]).then_inc(rest_w_loaded, 16)
            sp.dma_start(w1[:], att_w1).then_inc(att_loaded, 16)
            sp.dma_start(d2[:], dnn_w2).then_inc(dnn_loaded, 16)
            sp.dma_start(d3[:], dnn_w3).then_inc(dnn_loaded, 16)
            sp.dma_start(bias_rows[:], dnn_bias).then_inc(dnn_loaded, 16)
            sp.wait_ge(diag_cleared, 2)
            for j in range(G):
                block_j = slice(A * j, A * (j + 1))
                sp.dma_start(w2_diag[block_j, block_j], att_w2).then_inc(att_loaded, 16)
                sp.dma_start(w3_diag[block_j, j:j + 1], att_w3).then_inc(att_loaded, 16)

            for g in range(-(-T // G)):
                sp.wait_ge(score_ready, g + 1)
                for j in range(G):
                    count(sp, spread[j], 16 * g)
                sp.dma_start(score_dram, score[:]).then_inc(score_stored, 16)
                sp.wait_ge(score_stored, 16 * g + 16)
                count(sp, su_ready, G * g - G)
                for j in range(min(G, T - G * g)):
                    sp.dma_start(score_all[:, g % 2, j, :], score_dram[j:j + 1, :].broadcast_to([P, B]))\
                        .then_inc(spread[j], 16)
            sp.wait_ge(y_ready, 1)
            sp.dma_start(out, y[:]).then_inc(stored, 16)
            sp.wait_ge(stored, 16)

        @block.gpsimd
        def _(pool):
            nc.gpsimd.iota(idx_off[:], pattern=[[CANDS, T + 2], [0, NC]], base=0,
                           channel_multiplier=0).then_inc(offsets_made, 1)
            nc.gpsimd.memset(identity[:], 0.0).then_inc(identity_step, 1)
            pool.wait_ge(identity_step, 1)
            nc.gpsimd.affine_select(out=identity[:], in_=identity[:], compare_op=ALU.not_equal, fill=1.0,
                                    base=0, pattern=[[-1, P]], channel_multiplier=1).then_inc(identity_step, 1)

            def place_indices(i, k):
                half = (k // AHEAD) % 2
                if not (isinstance(i, int) and RING * i + k < 2 * AHEAD):
                    last = k - AHEAD - 1
                    pool.wait_ge(gathered[last % RING], 16 * NC * (i + last // RING + 1))
                nc.gpsimd.tensor_copy(idx_now[:, half], idx_all[:, bass.ds(RING * i + k, AHEAD), :])\
                    .then_inc(idx_copied, 1)

            def gather(i, k, chunks=range(NC)):
                for c in chunks:
                    nc.gpsimd.indirect_dma_start(
                        rows[:, k % RING, c, :], None, recent_emb,
                        bass.IndirectOffsetOnAxis(ap=idx_now[:, (k // AHEAD) % 2, k % AHEAD, c:c + 1], axis=0))\
                        .then_inc(gathered[k % RING], 16)

            def gather_fixed(f, table):
                for c in range(NC):
                    nc.gpsimd.indirect_dma_start(
                        fix_rows[:, f, c, :], None, table,
                        bass.IndirectOffsetOnAxis(ap=fix_idx[:, f, c:c + 1], axis=0)).then_inc(fix_gathered[f], 16)

            pool.wait_ge(idx_ready, 1)
            place_indices(0, 0)
            pool.wait_ge(idx_copied, 1)
            gather(0, 0)
            pool.wait_ge(idx_ready, 3)
            place_indices(0, AHEAD)
            pool.wait_ge(idx_copied, 2)
            for k in range(1, AHEAD):
                gather(0, k)
            gather_fixed(1, cand_emb)

            def step(i, k):
                t = RING * i + k
                if (k + 1) % AHEAD == 0 and exists(i, k + 1 + AHEAD):
                    place_indices(i, k + 1 + AHEAD)
                    pool.wait_ge(idx_copied, (RING // AHEAD) * i + (k + 1) // AHEAD + 2)
                if opening(i, k):
                    count(pool, h_ready, t + AHEAD - RING + 1)
                elif exists(i, k):
                    pool.wait_ge(z_ready, t + 1)
                    count(pool, h_ready, t)
                    nc.gpsimd.tensor_tensor(zh[:], z[:], h[:, (k - 1) % RING, :], ALU.mult).then_inc(zh_ready, 1)
                first_group = opening(i, k) and k == G - 1
                if exists(i, k + AHEAD) and not first_group:
                    gather(i, k + AHEAD, (0,))
                if exists(i, k - LAG):
                    s = t - LAG
                    cols = pieces(exists(i, k))[-1][0]
                    pool.wait_ge(spread[(k - LAG) % G], 16 * group(i, k - LAG) + 16)
                    pool.wait_ge(au_ready, s + 1)
                    nc.gpsimd.tensor_tensor(su[:, cols], au[:, cols],
                                            score_all[:, ((k - LAG) // G) % 2, (k - LAG) % G, cols],
                                            ALU.mult).then_inc(su_ready, 1)
                if exists(i, k) and not (opening(i, k) and k < G - 1):
                    if first_group:
                        pool.wait_ge(fix_copied, 1)
                    if k % G == 0:
                        pool.wait_ge(att1_done, group(i, k))
                    for j in range(2 if first_group else k, k + 1):
                        pool.wait_ge(h_ready, t - k + j + 1)
                        nc.gpsimd.tensor_tensor(hc[:, j % G, :], h[:, j % RING, :], cand_t[:], ALU.mult)\
                            .then_inc(hc_ready, 1)
                if exists(i, k + AHEAD):
                    gather(i, k + AHEAD, range(NC) if first_group else (1, 2, 3))
                if isinstance(i, int) and t == T - AHEAD:
                    gather_fixed(0, user_emb)

            run(pool, step)

        @block.scalar
        def _(act):
            def split_x(i, k):
                act.wait_ge(x_turned, RING * i + k + 1)
                nc.scalar.activation(x_hi[:, k % 2, :], ps_x[:], ACT.Copy).then_inc(x_hi_ready, 1)

            act.wait_ge(constants_set, 1)
            nc.scalar.activation(table_touch[:], eps[:], ACT.Sigmoid).then_inc(table_loaded, 1)
            act.wait_ge(table_loaded, 1)
            split_x(0, 0)
            act.wait_ge(small_loaded, 16)
            act.wait_ge(bias_ready, 4)

            def step(i, k):
                t = RING * i + k
                s = t - LAG
                gru, aug = exists(i, k), exists(i, k - LAG)
                if isinstance(i, int) and t == T:
                    act.wait_ge(fix_turned, 2)
                    nc.scalar.activation(user_t[:], ps_x[:], ACT.Copy).then_inc(fix_copied, 1)
                if gru:
                    act.wait_ge(r_done, t + 1)
                    nc.scalar.activation(r[:], ps_r[:], ACT.Sigmoid, bias=bias_r[:]).then_inc(r_ready, 1)
                if opening(i, k) and k == G - 1:
                    act.wait_ge(fix_turned, 1)
                    nc.scalar.activation(cand_t[:], ps_att[:], ACT.Copy).then_inc(fix_copied, 1)
                if ends_group(i, k - 2):
                    g = group(i, k - 2)
                    act.wait_ge(att3_done, g + 1)
                    count(act, score_stored, 16 * g)
                    nc.scalar.activation(score[:], ps_att[0:G, :], ACT.Sigmoid, bias=col(ATT_B3, G))\
                        .then_inc(score_ready, 1)
                if not opening(i, k) and exists(i, k + 1):
                    split_x(i, k + 1)
                if gru:
                    act.wait_ge(z_done, t + 1)
                    nc.scalar.activation(z[:], ps_z[:], ACT.Sigmoid, bias=bias_z[:]).then_inc(z_ready, 1)
                if opening(i, k) and k == 0:
                    split_x(0, 1)
                if gru:
                    act.wait_ge(n_pre_ready, t + 1)
                    nc.scalar.activation(n[:], n_pre[:], ACT.Tanh, bias=col(IH_N)).then_inc(n_ready, 1)
                if opening(i, k) and k < LAG - 1:
                    split_x(i, k + 2)
                if aug:
                    for p, (cols, reset, _) in enumerate(pieces(gru)):
                        act.wait_ge(ar_done, aug_count(s, p))
                        nc.scalar.activation(ar[:, cols], reset[:, cols], ACT.Sigmoid, bias=col(AUG_R)).then_inc(ar_ready, 1)
                if aug:
                    act.wait_ge(au_done, s + 1)
                    nc.scalar.activation(au[:], ps_au[:], ACT.Sigmoid, bias=col(AUG_U)).then_inc(au_ready, 1)
                if aug and gru:
                    act.wait_ge(rh_ready, s + 1)
                    nc.scalar.activation(rh_hi[:], rh[:], ACT.Copy).then_inc(rh_hi_ready, 1)
                if gru:
                    act.wait_ge(h_ready, t + 1)
                    nc.scalar.activation(h_hi[:, k % RING, :], h[:, k % RING, :], ACT.Copy).then_inc(h_hi_ready, 1)
                if ends_group(i, k - 1):
                    act.wait_ge(att2_done, group(i, k - 1) + 1)
                    nc.scalar.activation(att_p2[:], ps_att[:], ACT.Relu, bias=col(ATT_B2)).then_inc(p2_ready, 1)
                    nc.scalar.activation(att_n2[:], ps_att[:], ACT.Relu, bias=att_nb2[:], scale=-1.0).then_inc(n2_ready, 1)
                if aug:
                    for p, (cols, _, candidate) in enumerate(pieces(gru)):
                        act.wait_ge(ah_done, aug_count(s, p))
                        nc.scalar.activation(hhat[:, cols], candidate[:, cols], ACT.Tanh, bias=col(AUG_H))\
                            .then_inc(hhat_ready, 1)

            run(act, step)
            for layer, parts in ((0, P), (1, H2)):
                act.wait_ge(var_ready, layer + 1)
                nc.scalar.activation(std[0:parts], aggr[0:parts, 1:2], ACT.Sqrt, bias=eps[0:parts]).then_inc(std_ready, 1)

        @block.vector
        def _(dve):
            nc.vector.memset(eps[:], EPS).then_inc(constants_set, 1)
            nc.vector.memset(idx_all[:], 0).then_inc(idx_step, 1)
            nc.vector.memset(h[:, RING - 1, :], 0.0).then_inc(gru_zeroed, 1)
            nc.vector.memset(w2_diag[:], 0.0).then_inc(diag_cleared, 1)
            nc.vector.memset(w3_diag[:], 0.0).then_inc(diag_cleared, 1)
            nc.vector.memset(ones[:], 1.0).then_inc(constants_set, 1)

            steps = 1

            def idx_op(ins):
                nonlocal steps
                steps += 1
                ins.then_inc(idx_step, 1)
                dve.wait_ge(idx_step, steps)

            dve.wait_ge(idx_loaded, 16)
            for steps_ in (slice(0, AHEAD), slice(AHEAD, T)):
                raw, neg, flt = (a[:, steps_, :] for a in (idx_raw, idx_neg, idx_flt))
                idx_op(nc.vector.tensor_scalar(neg, raw, 0.0, float(CANDS), ALU.is_lt, ALU.mult))
                idx_op(nc.vector.tensor_tensor(flt, raw, neg, ALU.add))
                idx_op(nc.vector.tensor_scalar(flt, flt, 0.0, float(CANDS - 1), ALU.max, ALU.min))
                dve.wait_ge(offsets_made, 1)
                nc.vector.tensor_tensor(idx_all[:, steps_, :], flt, idx_off[:, steps_, :], ALU.add).then_inc(idx_ready, 1)
            dve.wait_ge(fix_idx_loaded, 32)
            for f, size in enumerate((USERS, CANDS)):
                idx_op(nc.vector.tensor_scalar(fix_neg[:, f, :], fix_raw[:, f, :], 0.0, float(size), ALU.is_lt, ALU.mult))
                idx_op(nc.vector.tensor_tensor(fix_flt[:, f, :], fix_raw[:, f, :], fix_neg[:, f, :], ALU.add))
                last = nc.vector.tensor_scalar(fix_idx[:, f, :], fix_flt[:, f, :], 0.0, float(size - 1), ALU.max, ALU.min)
            last.then_inc(idx_ready, 1)

            parts = (slice(0, INPUT), slice(INPUT, SPLIT))
            for part, arrived in zip(parts, (input_w_loaded, w_loaded)):
                dve.wait_ge(arrived, 16)
                nc.vector.tensor_copy(w_hi[:, part, :], w[:, part, :]).then_inc(setup_step, 1)
                dve.wait_ge(setup_step, 1 if part is parts[0] else 2)
                nc.vector.tensor_tensor(w_lo[:, part, :], w[:, part, :], w_hi[:, part, :].bitcast(fp32),
                                        ALU.subtract).then_inc(w_ready, 1)
            nc.vector.memset(ah[:, 1, :], 0.0).then_inc(aug_zeroed, 1)
            for state in (ah_hi, ah_lo):
                nc.vector.memset(state[:].bitcast(fp32), 0.0).then_inc(aug_zeroed, 1)

            def split_x(i, k):
                dve.wait_ge(x_hi_ready, RING * i + k + 1)
                nc.vector.tensor_tensor(x_lo[:, k % 2, :], ps_x[:], x_hi[:, k % 2, :].bitcast(fp32),
                                        ALU.subtract).then_inc(x_lo_ready, 1)

            dve.wait_ge(small_loaded, 16)
            nc.vector.tensor_tensor(bias_r[:], col(IH_R), col(HH_R), ALU.add).then_inc(bias_ready, 1)
            nc.vector.tensor_tensor(bias_z[:], col(IH_Z), col(HH_Z), ALU.add).then_inc(bias_ready, 1)
            nc.vector.tensor_scalar(att_nb2[:], col(ATT_B2), -1.0, None, ALU.mult).then_inc(bias_ready, 1)
            nc.vector.tensor_scalar(att_na2[:], col(ATT_A2), -1.0, None, ALU.mult).then_inc(bias_ready, 1)
            dve.wait_ge(att_loaded, 16 * (1 + 2 * G))
            nc.vector.tensor_tensor(w1_hs[:], w1[:, 0, :], w1[:, 2, :], ALU.add)
            for j in range(G):
                last = nc.vector.tensor_tensor(w1_c[:, j, :], w1[:, 1, :], w1[:, 2, :], ALU.subtract)
            last.then_inc(att_w_ready, 1)
            split_x(0, 0)

            def step(i, k):
                t = RING * i + k
                s = t - LAG
                gru, aug = exists(i, k), exists(i, k - LAG)
                slot = k % RING
                if gru:
                    dve.wait_ge(nh_done, t + 1)
                    dve.wait_ge(r_ready, t + 1)
                    nc.vector.scalar_tensor_tensor(out=rhn[:], in0=ps_nh[:], scalar=col(HH_N), in1=r[:],
                                                   op0=ALU.add, op1=ALU.mult).then_inc(rhn_ready, 1)
                    if exists(i, k - 1 - LAG):
                        last_aug = ah[:, (k - 1 - LAG) % 2, :]
                        dve.wait_ge(ah_ready, s)
                        nc.vector.tensor_copy(ah_hi[:], last_aug).then_inc(ah_hi_ready, 1)
                    dve.wait_ge(nx_done, t + 1)
                    dve.wait_ge(rhn_ready, t + 1)
                    nc.vector.tensor_tensor(n_pre[:], ps_nx[:], rhn[:], ALU.add).then_inc(n_pre_ready, 1)
                    if exists(i, k - 1 - LAG):
                        dve.wait_ge(ah_hi_ready, s)
                        nc.vector.tensor_tensor(ah_lo[:], last_aug, ah_hi[:].bitcast(fp32), ALU.subtract)\
                            .then_inc(ah_lo_ready, 1)
                    if not opening(i, k) and exists(i, k + 1):
                        split_x(i, k + 1)
                if opening(i, k) and k == 0:
                    split_x(0, 1)
                if opening(i, k):
                    dve.wait_ge(z_ready, t + 1)
                    nc.vector.tensor_tensor(zh[:], z[:], h[:, (k - 1) % RING, :], ALU.mult).then_inc(zh_ready, 1)
                    if k == G - 1:
                        dve.wait_ge(fix_copied, 1)
                        nc.vector.tensor_tensor(hc[:, 0, :], h[:, 0, :], cand_t[:], ALU.mult).then_inc(hc_ready, 1)
                if ends_group(i, k - 1):
                    g = group(i, k - 1)
                    dve.wait_ge(att1_done, g + 1)
                    if isinstance(i, int) and g == 0:
                        dve.wait_ge(att_c_ready, 1)
                    nc.vector.tensor_tensor(att_v1[:], ps_att[:], att_c[:], ALU.add).then_inc(v1_ready, 1)
                if gru:
                    dve.wait_ge(n_ready, t + 1)
                    nc.vector.scalar_tensor_tensor(out=zn[:], in0=z[:], scalar=1.0, in1=n[:],
                                                   op0=ALU.subtract, op1=ALU.mult).then_inc(zn_ready, 1)
                if ends_group(i, k - 1):
                    dve.wait_ge(v1_ready, g + 1)
                    nc.vector.tensor_scalar(att_n1[:], att_v1[:], 0.0, col(ATT_A1), ALU.min, ALU.mult).then_inc(n1_ready, 1)
                    dve.wait_ge(n1_ready, g + 1)
                    nc.vector.scalar_tensor_tensor(out=att_o1[:], in0=att_v1[:], scalar=0.0, in1=att_n1[:],
                                                   op0=ALU.max, op1=ALU.add).then_inc(o1_ready, 1)
                if aug:
                    old = ah[:, (k - LAG - 1) % 2, :]
                    for p, (cols, _, _) in enumerate(pieces(gru)):
                        dve.wait_ge(ar_ready, aug_count(s, p))
                        count(dve, ah_ready, aug_count(s - 1))
                        nc.vector.tensor_tensor(rh[:, cols], ar[:, cols], old[:, cols], ALU.mult).then_inc(rh_ready, 1)
                if gru:
                    dve.wait_ge(zh_ready, t + 1)
                    dve.wait_ge(zn_ready, t + 1)
                    nc.vector.tensor_tensor(h[:, slot, :], zh[:], zn[:], ALU.subtract).then_inc(h_ready, 1)
                if opening(i, k) and k < LAG - 1:
                    split_x(i, k + 2)
                if aug and gru:
                    dve.wait_ge(rh_hi_ready, s + 1)
                    nc.vector.tensor_tensor(rh_lo[:], rh[:], rh_hi[:].bitcast(fp32), ALU.subtract).then_inc(rh_lo_ready, 1)
                if gru:
                    dve.wait_ge(h_ready, t + 1)
                    dve.wait_ge(h_hi_ready, t + 1)
                    nc.vector.tensor_tensor(h_lo[:, slot, :], h[:, slot, :], h_hi[:, slot, :].bitcast(fp32),
                                            ALU.subtract).then_inc(h_lo_ready, 1)
                if opening(i, k) and k == G - 1:
                    nc.vector.tensor_tensor(hc[:, 1, :], h[:, 1, :], cand_t[:], ALU.mult).then_inc(hc_ready, 1)
                    dve.wait_ge(cand_done, 1)
                    nc.vector.tensor_scalar(att_c[:], ps_au[:], col(ATT_B1), None, ALU.add).then_inc(att_c_ready, 1)
                if ends_group(i, k - 1):
                    dve.wait_ge(p2_ready, g + 1)
                    dve.wait_ge(n2_ready, g + 1)
                    nc.vector.scalar_tensor_tensor(out=att_o2[:], in0=att_n2[:], scalar=att_na2[:], in1=att_p2[:],
                                                   op0=ALU.mult, op1=ALU.add).then_inc(o2_ready, 1)
                if aug:
                    new = ah[:, (k - LAG) % 2, :]
                    if not gru:
                        first_half = pieces(gru)[0][0]
                        dve.wait_ge(spread[(k - LAG) % G], 16 * group(i, k - LAG) + 16)
                        dve.wait_ge(au_ready, s + 1)
                        nc.vector.tensor_tensor(su0[:], au[:, first_half],
                                                score_all[:, ((k - LAG) // G) % 2, (k - LAG) % G, first_half],
                                                ALU.mult).then_inc(su0_ready, 1)
                    for p, (cols, _, _) in enumerate(pieces(gru)):
                        if not gru and p == 0:
                            scaled = su0[:]
                            dve.wait_ge(su0_ready, s - WHOLE + 1)
                        else:
                            scaled = su[:, cols]
                            dve.wait_ge(su_ready, s + 1)
                        nc.vector.scalar_tensor_tensor(out=keep[:, cols], in0=scaled, scalar=1.0, in1=old[:, cols],
                                                       op0=ALU.subtract, op1=ALU.mult).then_inc(keep_ready, 1)
                        dve.wait_ge(hhat_ready, aug_count(s, p))
                        nc.vector.tensor_tensor(take[:, cols], scaled, hhat[:, cols], ALU.mult).then_inc(take_ready, 1)
                    for p, (cols, _, _) in enumerate(pieces(gru)):
                        dve.wait_ge(keep_ready, aug_count(s, p))
                        dve.wait_ge(take_ready, aug_count(s, p))
                        nc.vector.tensor_tensor(new[:, cols], take[:, cols], keep[:, cols], ALU.subtract).then_inc(ah_ready, 1)

            run(dve, step)

            done = 0

            def link(ins):
                nonlocal done
                done += 1
                ins.then_inc(dnn_step, 1)
                dve.wait_ge(dnn_step, done)

            for layer, (parts, ps, ready, g_, b_, a, dst) in enumerate((
                    (P, ps_r, dnn1_done, BN1_G, BN1_B, DNN_A1, dz1),
                    (H2, ps_att, dnn2_done, BN2_G, BN2_B, DNN_A2, dz2))):
                on = slice(0, parts)
                dve.wait_ge(ready, 1)
                link(nc.vector.bn_stats(stats[on], ps[on]))
                nc.vector.bn_aggr(aggr[on], stats[on]).then_inc(var_ready, 1)
                dve.wait_ge(std_ready, layer + 1)
                link(nc.vector.reciprocal(rstd[on], std[on]))
                link(nc.vector.tensor_tensor(gain[on], rstd[on], col(g_, parts), ALU.mult))
                link(nc.vector.scalar_tensor_tensor(out=offset[on], in0=aggr[on, 0:1], scalar=gain[on],
                                                    in1=col(b_, parts), op0=ALU.mult, op1=ALU.subtract))
                for cols in HALVES:
                    link(nc.vector.tensor_scalar(dy[on, cols], ps[on, cols], gain[on], offset[on], ALU.mult, ALU.subtract))
                    link(nc.vector.tensor_scalar(dn[on, cols], dy[on, cols], 0.0, col(a, parts), ALU.min, ALU.mult))
                    nc.vector.scalar_tensor_tensor(out=dst[on, cols], in0=dy[on, cols], scalar=0.0, in1=dn[on, cols],
                                                   op0=ALU.max, op1=ALU.add).then_inc(dnn_made, 1)
            dve.wait_ge(dnn3_done, 1)
            nc.vector.tensor_scalar(y[:], ps_x[0:1, :], col(DNN_B3, 1), None, ALU.add).then_inc(y_ready, 1)

        @block.tensor
        def _(pe):
            mm = nc.tensor.matmul

            def turn(src, ps, semaphore):
                for c in range(NC):
                    last = nc.tensor.transpose(ps[:, c * P:(c + 1) * P], src[:, c, :], identity[:])
                last.then_inc(semaphore, 1)

            def turn_x(i, k):
                pe.wait_ge(gathered[k % RING], 16 * NC * (i + k // RING + 1))
                turn(rows[:, k % RING], ps_x, x_turned)

            def exact(ps, block_, hi, lo, start, stop, cols=slice(0, B)):
                mm(ps[:, cols], w_hi[:, block_, :], hi[:, cols], start=start, stop=False)
                mm(ps[:, cols], w_lo[:, block_, :], hi[:, cols], start=False, stop=False)
                return mm(ps[:, cols], w_hi[:, block_, :], lo[:, cols], start=False, stop=stop)

            def input_gate(i, k, ps, block_, read, closed):
                pe.wait_ge(x_lo_ready, RING * i + k + 1)
                count(pe, read, RING * i + k)
                return exact(ps, block_, x_hi[:, k % 2, :], x_lo[:, k % 2, :], True, closed)

            pe.wait_ge(w_loaded, 16)
            pe.wait_ge(gru_zeroed, 1)
            mm(ps_nh[:], w[:, W_HN, :], h[:, RING - 1, :], start=True, stop=True).then_inc(nh_done, 1)
            mm(ps_r[:], w[:, W_HR, :], h[:, RING - 1, :], start=True, stop=False)
            pe.wait_ge(identity_step, 2)
            turn_x(0, 0)
            mm(ps_z[:], w[:, W_HZ, :], h[:, RING - 1, :], start=True, stop=False)
            pe.wait_ge(w_ready, 2)
            pe.wait_ge(x_lo_ready, 1)
            exact(ps_r, W_IR, x_hi[:, 0, :], x_lo[:, 0, :], False, True).then_inc(r_done, 1)
            exact(ps_z, W_IZ, x_hi[:, 0, :], x_lo[:, 0, :], False, True).then_inc(z_done, 1)
            exact(ps_nx, W_IN, x_hi[:, 0, :], x_lo[:, 0, :], True, True).then_inc(nx_done, 1)
            turn_x(0, 1)
            pe.wait_ge(att_w_ready, 1)
            pe.wait_ge(rest_w_loaded, 16)
            pe.wait_ge(aug_zeroed, 3)

            def attention_1(i, k):
                states = [(k - k % G + j) % RING for j in range(G)]
                tiles = [ps_att[A * j:A * (j + 1), :] for j in range(G)]
                count(pe, score_ready, group(i, k))
                pe.wait_ge(hc_ready, RING * i + k + 1)
                for tile, state in zip(tiles, states):
                    mm(tile, w1_hs[:], h[:, state, :], start=True, stop=False)
                for j, tile in enumerate(tiles):
                    last = mm(tile, w1[:, 3, :], hc[:, j, :], start=False, stop=True)
                last.then_inc(att1_done, 1)

            def attention_2(i, k):
                pe.wait_ge(o1_ready, group(i, k) + 1)
                mm(ps_att[:], w2_diag[:], att_o1[:], start=True, stop=True).then_inc(att2_done, 1)

            def attention_3(i, k):
                pe.wait_ge(o2_ready, group(i, k) + 1)
                mm(ps_att[0:G, :], w3_diag[:], att_o2[:], start=True, stop=True).then_inc(att3_done, 1)

            def opening_step(i, k):
                prev = (k - 1) % RING
                if k > 0:
                    pe.wait_ge(h_ready, k)
                    mm(ps_r[:], w[:, W_HR, :], h[:, prev, :], start=False, stop=True).then_inc(r_done, 1)
                    mm(ps_nh[:], w[:, W_HN, :], h[:, prev, :], start=True, stop=True).then_inc(nh_done, 1)
                    mm(ps_z[:], w[:, W_HZ, :], h[:, prev, :], start=False, stop=True).then_inc(z_done, 1)
                if k == G - 1:
                    pe.wait_ge(fix_copied, 1)
                    mm(ps_au[:], w1_c[:].rearrange("p g a -> p (g a)"), cand_t[:], start=True, stop=True)\
                        .then_inc(cand_done, 1)
                if k == G:
                    attention_1(i, k - 1)
                input_gate(i, k + 1, ps_r, W_IR, r_ready, False)
                if k < LAG - 1:
                    input_gate(i, k + 1, ps_nx, W_IN, n_pre_ready, True).then_inc(nx_done, 1)
                input_gate(i, k + 1, ps_z, W_IZ, z_ready, False)
                if k == G - 2:
                    pe.wait_ge(fix_gathered[1], 16 * NC)
                    turn(fix_rows[:, 1], ps_att, fix_turned)
                pe.wait_ge(x_lo_ready, k + 2)
                turn_x(i, k + 2)
                if k == G:
                    attention_2(i, k - 1)

            def steady_step(i, k):
                t = RING * i + k
                s = t - LAG
                hi, lo = h_hi[:, (k - 1) % RING, :], h_lo[:, (k - 1) % RING, :]
                state_hi, state_lo = h_hi[:, (k - LAG) % RING, :], h_lo[:, (k - LAG) % RING, :]
                pe.wait_ge(h_hi_ready, t)
                mm(ps_r[:], w_hi[:, W_HR, :], hi, start=False, stop=False)
                mm(ps_r[:], w_lo[:, W_HR, :], hi, start=False, stop=False)
                pe.wait_ge(h_lo_ready, t)
                mm(ps_r[:], w_hi[:, W_HR, :], lo, start=False, stop=True).then_inc(r_done, 1)
                first_aug = isinstance(i, int) and t == LAG
                if ends_group(i, k - 2) and not first_aug:
                    attention_3(i, k - 2)
                pe.wait_ge(rhn_ready, t)
                exact(ps_nh, W_HN, hi, lo, True, True).then_inc(nh_done, 1)
                if first_aug:
                    attention_3(i, k - 2)
                input_gate(i, k, ps_nx, W_IN, n_pre_ready, True).then_inc(nx_done, 1)
                exact(ps_z, W_HZ, hi, lo, False, True).then_inc(z_done, 1)
                if ends_group(i, k - 1):
                    attention_1(i, k - 1)
                count(pe, hhat_ready, s)
                exact(ps_a, W_ARX, state_hi, state_lo, True, False)
                count(pe, ah_hi_ready, s)
                mm(ps_a[:], w_hi[:, W_ARH, :], ah_hi[:], start=False, stop=False)
                mm(ps_a[:], w_lo[:, W_ARH, :], ah_hi[:], start=False, stop=False)
                count(pe, au_ready, s)
                exact(ps_au, W_AUX, state_hi, state_lo, True, False)
                count(pe, ah_lo_ready, s)
                mm(ps_a[:], w_hi[:, W_ARH, :], ah_lo[:], start=False, stop=True).then_inc(ar_done, 1)
                exact(ps_au, W_AUH, ah_hi[:], ah_lo[:], False, True).then_inc(au_done, 1)
                if exists(i, k + 1):
                    input_gate(i, k + 1, ps_r, W_IR, r_ready, False)
                if ends_group(i, k - 1):
                    attention_2(i, k - 1)
                pe.wait_ge(ar_ready, s + 1)
                exact(ps_a, W_AHX, state_hi, state_lo, True, False)
                if exists(i, k + 1):
                    input_gate(i, k + 1, ps_z, W_IZ, z_ready, False)
                pe.wait_ge(rh_hi_ready, s + 1)
                mm(ps_a[:], w_hi[:, W_AHH, :], rh_hi[:], start=False, stop=False)
                mm(ps_a[:], w_lo[:, W_AHH, :], rh_hi[:], start=False, stop=False)
                pe.wait_ge(rh_lo_ready, s + 1)
                mm(ps_a[:], w_hi[:, W_AHH, :], rh_lo[:], start=False, stop=True).then_inc(ah_done, 1)
                if exists(i, k + 2):
                    pe.wait_ge(x_lo_ready, t + 2)
                    turn_x(i, k + 2)

            def closing_step(i, k):
                t = RING * i + k
                s = t - LAG
                halves = pieces(False)
                old = ah[:, (k - LAG - 1) % 2, :]
                state_hi, state_lo = h_hi[:, (k - LAG) % RING, :], h_lo[:, (k - LAG) % RING, :]
                if t == T:
                    pe.wait_ge(fix_gathered[0], 16 * NC)
                    turn(fix_rows[:, 0], ps_x, fix_turned)
                if t == T + 1:
                    pe.wait_ge(fix_copied, 2)
                    pe.wait_ge(dnn_loaded, 48)
                    pe.wait_ge(constants_set, 2)
                    mm(ps_r[:], bias_rows[:, 0:P], ones[:], start=True, stop=False)
                    mm(ps_r[:], w[:, W_DU, :], user_t[:], start=False, stop=False)
                    mm(ps_r[:], w[:, W_DC, :], cand_t[:], start=False, stop=False)
                pe.wait_ge(au_ready, s)
                exact(ps_au, W_AUX, state_hi, state_lo, True, False)
                if ends_group(i, k - 2):
                    attention_3(i, k - 2)
                pe.wait_ge(hhat_ready, WHOLE)
                pe.wait_ge(ar_ready, aug_count(s - 1))
                for cols, reset, _ in halves:
                    exact(reset, W_ARX, state_hi, state_lo, True, False, cols)
                if ends_group(i, k - 1):
                    attention_1(i, k - 1)
                for p, (cols, reset, _) in enumerate(halves):
                    pe.wait_ge(ah_ready, aug_count(s - 1, p))
                    mm(reset[:, cols], w[:, W_ARH, :], old[:, cols], start=False, stop=True).then_inc(ar_done, 1)
                    last = mm(ps_au[:, cols], w[:, W_AUH, :], old[:, cols], start=False, stop=p == 1)
                last.then_inc(au_done, 1)
                pe.wait_ge(hhat_ready, aug_count(s - 1))
                for cols, _, candidate in halves:
                    exact(candidate, W_AHX, state_hi, state_lo, True, False, cols)
                for p, (cols, _, candidate) in enumerate(halves):
                    pe.wait_ge(rh_ready, aug_count(s, p))
                    mm(candidate[:, cols], w[:, W_AHH, :], rh[:, cols], start=False, stop=True).then_inc(ah_done, 1)
                if ends_group(i, k - 1):
                    attention_2(i, k - 1)

            def step(i, k):
                if opening(i, k):
                    opening_step(i, k)
                elif exists(i, k):
                    steady_step(i, k)
                else:
                    closing_step(i, k)

            run(pe, step)
            pe.wait_ge(score_ready, -(-T // G))
            mm(ps_att[0:H2, :], bias_rows[:, P:P + H2], ones[:], start=True, stop=False)
            for p, cols in enumerate(HALVES):
                pe.wait_ge(ah_ready, aug_count(T - 1, p))
                last = mm(ps_r[:, cols], w[:, W_DH, :], ah[:, (T - 1) % 2, cols], start=False, stop=p == 1)
            last.then_inc(dnn1_done, 1)
            for p, cols in enumerate(HALVES):
                pe.wait_ge(dnn_made, p + 1)
                last = mm(ps_att[0:H2, cols], d2[:], dz1[:, cols], start=False, stop=p == 1)
            last.then_inc(dnn2_done, 1)
            for p, cols in enumerate(HALVES):
                pe.wait_ge(dnn_made, p + 3)
                last = mm(ps_x[0:1, cols], d3[:], dz2[:, cols], start=True, stop=True)
            last.then_inc(dnn3_done, 1)


def kernel(**inputs):
    import numpy as np
    import concourse.bacc as bacc
    from concourse.bass_utils import run_bass_kernel_spmd

    x = {name.replace("L0_rec_", ""): np.asarray(a) for name, a in inputs.items()}

    def rows_of(a, n):
        return a.reshape(n, P, a.shape[1]).transpose(1, 0, 2)

    def chunks(idx):
        return np.ascontiguousarray(idx.reshape(NC, P, -1).transpose(1, 2, 0))

    ih, hh = rows_of(x["gru_W_ih"], 3), rows_of(x["gru_W_hh"], 3)
    wr, wu, wh = (rows_of(x[k], 2) for k in ("aug_Wr", "aug_Wu", "aug_Wh"))
    dnn = rows_of(x["dnn_W1"], 3)
    weights = np.empty((P, WEIGHTS, P), np.float32)
    for block, a in ((W_IR, ih[:, 0].T), (W_IZ, ih[:, 1].T), (W_IN, ih[:, 2].T),
                     (W_HR, hh[:, 0].T), (W_HZ, hh[:, 1].T), (W_HN, hh[:, 2].T),
                     (W_ARX, wr[:, 0]), (W_ARH, wr[:, 1]), (W_AUX, wu[:, 0]), (W_AUH, wu[:, 1]),
                     (W_AHH, wh[:, 0]), (W_AHX, wh[:, 1]), (W_DU, dnn[:, 0]), (W_DC, dnn[:, 1]), (W_DH, dnn[:, 2])):
        weights[:, block] = a
    small = np.zeros((P, SMALL), np.float32)
    for c, a in ((IH_R, x["gru_b_ih"][0:P]), (IH_Z, x["gru_b_ih"][P:2 * P]), (IH_N, x["gru_b_ih"][2 * P:]),
                 (HH_R, x["gru_b_hh"][0:P]), (HH_Z, x["gru_b_hh"][P:2 * P]), (HH_N, x["gru_b_hh"][2 * P:]),
                 (AUG_R, x["aug_br"]), (AUG_U, x["aug_bu"]), (AUG_H, x["aug_bh"]),
                 (BN1_G, x["bn1_g"]), (BN1_B, x["bn1_b"]),
                 (ATT_B1, np.tile(x["att_b1"], G)), (ATT_B2, np.tile(x["att_b2"], G)),
                 (BN2_G, x["bn2_g"]), (BN2_B, x["bn2_b"])):
        small[0:a.shape[0], c] = a
    for c, name in ((ATT_A1, "att_a1"), (ATT_A2, "att_a2"), (DNN_A1, "dnn_a1"), (DNN_A2, "dnn_a2"),
                    (ATT_B3, "att_b3"), (DNN_B3, "dnn_b3")):
        small[:, c] = x[name].reshape(())
    arrays = {
        "recent_idx": chunks(x["r_recent_features"]),
        "user_idx": chunks(x["r_user_features"])[:, 0],
        "cand_idx": chunks(x["r_candidate_features"])[:, 0],
        "user_emb": x["user_emb"],
        "cand_emb": x["cand_emb"],
        "recent_emb": x["recent_emb"].reshape(T * CANDS, P),
        "weights": weights,
        "small": small,
        "att_w1": rows_of(x["att_W1"], 4),
        "att_w2": x["att_W2"],
        "att_w3": x["att_W3"],
        "dnn_w2": x["dnn_W2"],
        "dnn_w3": x["dnn_W3"],
        "dnn_bias": np.concatenate((x["dnn_b1"], x["dnn_b2"]))[None],
    }
    arrays = {name: np.ascontiguousarray(a) for name, a in arrays.items()}

    nc = bacc.Bacc("TRN2", target_bir_lowering=False, num_devices=1)
    aps = {name: nc.dram_tensor(name, a.shape, mybir.dt.from_np(a.dtype), kind="ExternalInput").ap()
           for name, a in arrays.items()}
    out = nc.dram_tensor("out", (1, B), mybir.dt.float32, kind="ExternalOutput").ap()
    recommender(nc, **aps, out=out)
    result = run_bass_kernel_spmd(nc, [arrays], core_ids=[0])
    return result.results[0]["out"].reshape(B, 1)
```
